# Optimizing a Trainium2 kernel written in Bass

```python
import numpy as np
import jax
import jax.numpy as jnp

def _softmax(x, axis=-1):
    return jax.nn.softmax(x, axis=axis)

def _gelu(x):
    return jax.nn.gelu(x, approximate=True)

def _silu(x):
    return jax.nn.silu(x)

def _sigmoid(x):
    return jax.nn.sigmoid(x)

def _layernorm(x, axis=-1, eps=1e-05):
    m = jnp.mean(x, axis=axis, keepdims=True)
    v = jnp.var(x, axis=axis, keepdims=True)
    return (x - m) / jnp.sqrt(v + eps)

def _scatter_add(tgt, idx, src, axis=0):
    return tgt.at[idx].add(src)

def _segment_sum(src, seg, n):
    return jax.ops.segment_sum(src, seg, n)
kernel_name = 'mk_macaron_d1_jaxref_r8_58b2b0'

def setup_inputs(seed: int=0):
    np.random.seed(seed)
    _w = jnp.asarray

    def _L0_attn_setup():
        import jax, jax.numpy as jnp
        import numpy as np
        N_HEAD = 16
        D_MODEL = 128

        def _layernorm(y, gamma, beta, eps=1e-05):
            mu = jnp.mean(y, axis=-1, keepdims=True)
            var = jnp.var(y, axis=-1, keepdims=True)
            return (y - mu) * jax.lax.rsqrt(var + eps) * gamma + beta
        key = jax.random.key(seed)
        ks = jax.random.split(key, 7)
        s = 1.0 / np.sqrt(D_MODEL)
        x = jax.random.normal(ks[0], (4, 256, D_MODEL), dtype=jnp.float32)
        Wq = jax.random.uniform(ks[1], (D_MODEL, D_MODEL), jnp.float32, -s, s)
        Wk = jax.random.uniform(ks[2], (D_MODEL, D_MODEL), jnp.float32, -s, s)
        Wv = jax.random.uniform(ks[3], (D_MODEL, D_MODEL), jnp.float32, -s, s)
        bq = jax.random.uniform(ks[4], (D_MODEL,), jnp.float32, -s, s)
        bk = jax.random.uniform(ks[5], (D_MODEL,), jnp.float32, -s, s)
        bv = jax.random.uniform(ks[6], (D_MODEL,), jnp.float32, -s, s)
        gamma = jnp.ones((D_MODEL,), jnp.float32)
        beta = jnp.zeros((D_MODEL,), jnp.float32)
        return {'x': x, 'Wq': Wq, 'bq': bq, 'Wk': Wk, 'bk': bk, 'Wv': Wv, 'bv': bv, 'gamma': gamma, 'beta': beta}
    _L0_attn_in = _L0_attn_setup()

    def _L0_ffn_setup():
        import jax, jax.numpy as jnp
        import numpy as np
        import math
        D_IN = 128
        FEATURES = (512, 512, 128)
        BATCH, SEQ = (8, 256)

        def _conn_dense(kernel_bool, x):
            w = jnp.where(kernel_bool, jnp.float32(1.0), jnp.float32(-1.0))
            return x @ w
        key = jax.random.key(seed)
        kx, kk0, kk1, kk2 = jax.random.split(key, 4)
        x = jax.random.normal(kx, (BATCH, SEQ, D_IN), dtype=jnp.float32)
        k0 = jax.random.randint(kk0, (2 * D_IN, FEATURES[0]), 0, 2).astype(jnp.bool_)
        k1 = jax.random.randint(kk1, (FEATURES[0], FEATURES[1]), 0, 2).astype(jnp.bool_)
        k2 = jax.random.randint(kk2, (FEATURES[1], FEATURES[2]), 0, 2).astype(jnp.bool_)
        s0 = jnp.asarray(1.0 / math.sqrt(2 * D_IN), dtype=jnp.float32)
        s1 = jnp.asarray(1.0 / math.sqrt(FEATURES[0]), dtype=jnp.float32)
        s2 = jnp.asarray(1.0 / math.sqrt(FEATURES[1]), dtype=jnp.float32)
        return {'x': x, 'k0': k0, 'k1': k1, 'k2': k2, 's0': s0, 's1': s1, 's2': s2}
    _L0_ffn_in = _L0_ffn_setup()
    _d = {'L0_attn_x': _L0_attn_in['x'], 'L0_attn_Wq': _L0_attn_in['Wq'], 'L0_attn_bq': _L0_attn_in['bq'], 'L0_attn_Wk': _L0_attn_in['Wk'], 'L0_attn_bk': _L0_attn_in['bk'], 'L0_attn_Wv': _L0_attn_in['Wv'], 'L0_attn_bv': _L0_attn_in['bv'], 'L0_attn_gamma': _L0_attn_in['gamma'], 'L0_attn_beta': _L0_attn_in['beta'], 'L0_ffn_k0': _L0_ffn_in['k0'], 'L0_ffn_k1': _L0_ffn_in['k1'], 'L0_ffn_k2': _L0_ffn_in['k2'], 'L0_ffn_s0': _L0_ffn_in['s0'], 'L0_ffn_s1': _L0_ffn_in['s1'], 'L0_ffn_s2': _L0_ffn_in['s2']}
    _x0 = _d['L0_attn_x']
    _d['L0_attn_x'] = jax.random.normal(jax.random.fold_in(jax.random.key(seed), 1), (32, 256, 128), dtype=_x0.dtype)
    del _x0
    return _d

def reference(L0_attn_x, L0_attn_Wq, L0_attn_bq, L0_attn_Wk, L0_attn_bk, L0_attn_Wv, L0_attn_bv, L0_attn_gamma, L0_attn_beta, L0_ffn_k0, L0_ffn_k1, L0_ffn_k2, L0_ffn_s0, L0_ffn_s1, L0_ffn_s2):

    def _L0_attn_ref(x, Wq, bq, Wk, bk, Wv, bv, gamma, beta):
        import jax, jax.numpy as jnp
        import numpy as np
        N_HEAD = 16
        D_MODEL = 128

        def _layernorm(y, gamma, beta, eps=1e-05):
            mu = jnp.mean(y, axis=-1, keepdims=True)
            var = jnp.var(y, axis=-1, keepdims=True)
            return (y - mu) * jax.lax.rsqrt(var + eps) * gamma + beta
        b, s, d = x.shape
        h = N_HEAD
        hd = d // h

        def proj(W, bias):
            return (x @ W.T + bias).reshape(b, s, h, hd).transpose(0, 2, 1, 3)
        Q = proj(Wq, bq)
        K = proj(Wk, bk)
        V = proj(Wv, bv)
        scale = 1.0 / np.sqrt(hd)
        attn = jnp.einsum('bhqd,bhkd->bhqk', Q, K) * scale
        attn = jax.nn.softmax(attn, axis=-1)
        ctx = jnp.einsum('bhqk,bhkd->bhqd', attn, V)
        ctx = ctx.transpose(0, 2, 1, 3).reshape(b, s, d)
        return _layernorm(ctx + x, gamma, beta)

    def _L0_ffn_ref(x, k0, k1, k2, s0, s1, s2):
        import jax, jax.numpy as jnp
        import numpy as np
        import math
        D_IN = 128
        FEATURES = (512, 512, 128)
        BATCH, SEQ = (8, 256)

        def _conn_dense(kernel_bool, x):
            w = jnp.where(kernel_bool, jnp.float32(1.0), jnp.float32(-1.0))
            return x @ w
        h = jnp.concatenate([x, -x], axis=-1)
        h = s0 * _conn_dense(k0, h)
        h = jax.nn.relu(h) * 2
        h = s1 * _conn_dense(k1, h)
        h = jax.nn.relu(h) * 2
        h = s2 * _conn_dense(k2, h)
        return h
    x = L0_attn_x
    x = x + 0.5 * _L0_ffn_ref(_layernorm(x, axis=-1), L0_ffn_k0, L0_ffn_k1, L0_ffn_k2, L0_ffn_s0, L0_ffn_s1, L0_ffn_s2)
    x = x + _L0_attn_ref(_layernorm(x, axis=-1), L0_attn_Wq, L0_attn_bq, L0_attn_Wk, L0_attn_bk, L0_attn_Wv, L0_attn_bv, L0_attn_gamma, L0_attn_beta)
    x = x + 0.5 * _L0_ffn_ref(_layernorm(x, axis=-1), L0_ffn_k0, L0_ffn_k1, L0_ffn_k2, L0_ffn_s0, L0_ffn_s1, L0_ffn_s2)
    return x

_drawn_inputs = setup_inputs


def setup_inputs(seed=0):
    import zlib

    import numpy as np

    out = dict(_drawn_inputs(seed))
    spreads = {'L0_attn_gamma': (1.0, 0.2), 'L0_attn_beta': (0.0, 0.1)}
    factors = {'L0_attn_Wq': 8.0,
     'L0_attn_bq': 8.0,
     'L0_attn_Wk': 8.0,
     'L0_attn_bk': 8.0,
     'L0_attn_bv': 2.924}
    for name, (base, spread) in spreads.items():
        noise = np.random.default_rng([zlib.crc32(name.encode()), seed]).standard_normal(out[name].shape)
        drawn = base * np.exp(spread * noise) if base else spread * noise
        out[name] = jnp.asarray(drawn.astype(out[name].dtype))
    for name, factor in factors.items():
        out[name] = (out[name] * factor).astype(out[name].dtype)
    return out
```

```python
import numpy as np
from contextlib import ExitStack

import concourse.bass as bass
from concourse import mybir
from concourse.alu_op_type import AluOpType as ALU

F32 = mybir.dt.float32
F16 = mybir.dt.float16
U8 = mybir.dt.uint8
ACT = mybir.ActivationFunctionType
AX = mybir.AxisListType
RMAX = bass.bass_isa.ReduceOp.max

P = 128
SEQ = 256
TILE = 512
TT = TILE // P
HEADS, HD = 16, 8
GROUPS, LANES = 4, 4
ROWS = 32
PARTS = 3
UNITS = 32
HALF = 16
HB = 8
HIDDEN = 512
KC = HIDDEN // P
EPS = 1e-5
XN_SCALE = 2.0 ** 8
W0_UNIT = 0.5
W1_UNIT = 2.0 ** -8
Q_MAX = 2.0 ** 13
M_UNIT = 2.0 ** -14
FFN_OUT = 0.5 * 2 * 2 / (XN_SCALE * W0_UNIT / 2 * W1_UNIT)

MISC = [("MT3", 1), ("CT00", 3), ("CT01", 4), ("LNT", 7), ("Q", 8), ("MT0", 9), ("K", 10),
        ("MT1", 17), ("V", 18), ("CT10", 19), ("CT11", 20), ("MT2", 25)]
PREP_USES = ("LNT", "Q", "K", "V")
Z_USES = 10
SPREADS = 2 * LANES * PARTS
AT_LNT, AT_Q, AT_K, AT_V = 7, 8, 10, 18
AT_STATS_PREP, AT_STATS_B, AT_STATS_A = 3, 11, 28


class Iteration:

    def __init__(self, t, par, cur=True, prev=True, prep=True, ffn_a=None, ffn_b=None,
                 next_a=None, misc_base=None):
        self.t, self.par, self.cur, self.prev, self.prep = t, par, cur, prev, prep
        self.ffn_a, self.ffn_b = ffn_a, ffn_b
        self.next_a = next_a
        names = [n for n, _ in MISC if
                 (n in PREP_USES and prep) or (n in ("MT0", "MT1", "MT2") and cur)
                 or (n in ("MT3", "CT00", "CT01", "CT10", "CT11") and prev)]
        self.misc = {n: misc_base + i for i, n in enumerate(names)}


def macaron_layer(nc, x, wq, bq, wk, bk, wv, bv, gamma, beta, k0, k1, k2, s0, s1, s2, out):
    tokens = x.shape[0] * x.shape[1]
    TILES = tokens // TILE
    x_flat = x.rearrange("n s d -> (n s d)")
    out_flat = out.rearrange("n s d -> (n s d)")

    with ExitStack() as ctx:
        def sb(name, shape, dt=F32):
            return ctx.enter_context(nc.sbuf_tensor(name, shape, dt))

        def bank(name):
            return ctx.enter_context(nc.psum_tensor(name, [P, TILE], F32))

        def sem(name):
            return ctx.enter_context(nc.semaphore(name))

        ident = sb("ident", [P, P])
        ident16 = sb("ident16", [P, P], F16)
        k0_raw = sb("k0_raw", [P, 2, HIDDEN], U8)
        k1_raw = sb("k1_raw", [P, KC, HIDDEN], U8)
        k2_raw = sb("k2_raw", [P, KC, P], U8)
        w0 = sb("w0", [P, HIDDEN], F16)
        w0_diff = sb("w0_diff", [P, HIDDEN], F16)
        w1 = sb("w1", [P, KC, HIDDEN], F16)
        w2 = sb("w2", [P, KC, P], F16)
        s_raw = sb("s_raw", [P, 3])
        s_sign = sb("s_sign", [P, 2])
        s_tmp = sb("s_tmp", [P, 4])
        w0_scale = sb("w0_scale", [P, 1])
        w1_scale = sb("w1_scale", [P, 2])
        ffn_scale = sb("ffn_scale", [P, 1])
        w_raw = sb("w_raw", [P, 3, P])
        w_sq = sb("w_sq", [P, 3, P])
        w_fit = sb("w_fit", [P, 3, P])
        b_raw = sb("b_raw", [P, 3])
        b_abs = sb("b_abs", [P, 3])
        b_fit = sb("b_fit", [P, 3])
        w_norm = sb("w_norm", [P, 3])
        w_bound = sb("w_bound", [P, 3])
        w_most = sb("w_most", [P, 3])
        w_inv = sb("w_inv", [P, 3])
        w_factor = sb("w_factor", [P, 3])
        score_tmp = sb("score_tmp", [P, 1])
        score_scale = sb("score_scale", [P, 1])
        v_unscale = sb("v_unscale", [P, 1])
        wt_hi = sb("wt_hi", [P, 3, P], F16)
        wt_lo = sb("wt_lo", [P, 3, P], F16)
        gamma_b = sb("gamma_b", [P, P])
        beta_b = sb("beta_b", [P, P])
        bv_b = sb("bv_b", [P, P])
        minus_half = sb("minus_half", [P, TT])
        plus_half = sb("plus_half", [P, 3])
        eps = sb("eps", [P, TT])
        x0 = sb("x0", [P, TT, P])
        x1 = [sb(f"x1_{i}", [P, TT, P]) for i in range(2)]
        x2 = [sb(f"x2_{i}", [P, TT, P]) for i in range(2)]
        x3 = sb("x3", [P, TT, P])
        ffn_bn = sb("ffn_bn", [P, TT, 6])
        ffn_mv = sb("ffn_mv", [P, TT, 2])
        ffn_xc = sb("ffn_xc", [P, TT, P])
        ffn_ve = sb("ffn_ve", [P, TT])
        ffn_rs = sb("ffn_rs", [P, TT])
        ffn_xn = sb("ffn_xn", [P, TT, P])
        ffn_hi = sb("ffn_hi", [P, 9, TILE], F16)
        ffn_lo = sb("ffn_lo", [P, 9, TILE], F16)
        att_bn = sb("att_bn", [P, TT, 6])
        att_mv = sb("att_mv", [P, TT, 2])
        att_xc = sb("att_xc", [P, TT, P])
        att_ve = sb("att_ve", [P, TT])
        att_rs = sb("att_rs", [P, TT])
        att_xn = [sb(f"att_xn{i}", [P, TT, P]) for i in range(2)]
        att_hi = sb("att_hi", [P, TILE], F16)
        att_lo = sb("att_lo", [P, TILE], F16)
        qk_hi = [sb(f"{n}_hi", [P, TILE], F16) for n in "qk"]
        qk_lo = [sb(f"{n}_lo", [P, TILE], F16) for n in "qk"]
        q_rows = [sb(f"q_rows{i}", [P, GROUPS, TILE], F16) for i in range(2)]
        k_rows = [sb(f"k_rows{i}", [P, GROUPS, TILE], F16) for i in range(2)]
        v_cols = [sb(f"v_cols{i}", [P, TT, HEADS, ROWS]) for i in range(2)]
        row_max = sb("row_max", [P, 2 * LANES, 2])
        max_parts = sb("max_parts", [P, 2 * LANES, 2, 2], F16)
        max_rows = sb("max_rows", [4 * LANES, SEQ], F16)
        probs = [sb(f"probs{i}", [P, LANES, TILE]) for i in range(2)]
        ctx_t = sb("ctx_t", [P, GROUPS, SEQ])
        den = sb("den", [P, HEADS])
        ctx_n = sb("ctx_n", [P, 2, P])
        att_y = sb("att_y", [P, 2, P])
        tail_bn = sb("tail_bn", [P, 2, 6])
        tail_mv = sb("tail_mv", [P, 2, 2])
        tail_xc = sb("tail_xc", [P, 2, P])
        tail_ve = sb("tail_ve", [P, 2])
        tail_rs = sb("tail_rs", [P, 2])
        tail_n = sb("tail_n", [P, 2, P])
        tail_g = sb("tail_g", [P, 2, P])
        xn_bv = sb("xn_bv", [P, TT, P])
        x1_beta = sb("x1_beta", [P, TT, P])

        ps_z = [bank(f"ps_z{i}") for i in range(2)]
        ps_s = [bank(f"ps_s{i}") for i in range(2)]
        ps_t = [bank(f"ps_t{i}") for i in range(2)]
        ps_c = bank("ps_c")
        ps_m = bank("ps_m")

        s_params = sem("params_loaded")
        s_x0 = sem("x0_loaded")
        s_out = sem("out_stored")
        s_const = sem("consts_made")
        s_setd = sem("setup_vector")
        s_setp = sem("setup_pool")
        s_wt = sem("wt_transposed")
        s_wthi = sem("wt_hi_made")
        f_bn, f_mv, f_rs, f_xn = sem("ffn_bn_done"), sem("ffn_mv_done"), sem("ffn_rstd_steps"), sem("ffn_xn_done")
        z_full, z_hi, z_free = sem("z_full"), sem("z_hi_made"), sem("z_free")
        a_bn, a_mv, a_rs, a_xn = sem("att_bn_done"), sem("att_mv_done"), sem("att_rstd_steps"), sem("att_xn_done")
        m_full, m_hi, m_free = sem("misc_full"), sem("misc_hi_made"), sem("misc_free")
        s_spread = sem("rows_spread")
        s_full, s_max = sem("scores_full"), sem("max_done")
        s_mparts = sem("max_parts_made")
        s_mrows = sem("max_rows_placed")
        t_full, s_exp = sem("shifted_scores_full"), sem("exp_done")
        c_full, c_free = sem("context_full"), sem("context_copied")
        s_den = sem("den_inverted")
        s_y = sem("att_y_done")
        t_bn, t_mv, t_rs = sem("tail_bn_done"), sem("tail_mv_done"), sem("tail_rstd_steps")
        t_n = sem("tail_steps")
        s_x2 = sem("x2_done")
        s_base = sem("tail_base_done")

        def full(t, r):
            return Iteration(t, r, ffn_a=2 * t, ffn_b=2 * t + 1, next_a=2 * t + 2, misc_base=12 * t - 1)

        head = [Iteration(0, 0, prev=False, ffn_b=2, misc_base=4),
                Iteration(1, 1, ffn_b=3, next_a=4, misc_base=11)]
        LOOP_FROM, LOOP_TO = 2, TILES - 2
        T = TILES
        tail = [Iteration(T - 2, 0, ffn_a=2 * (T - 2), next_a=2 * (T - 2) + 1, misc_base=12 * (T - 2) - 1),
                Iteration(T - 1, 1, prep=False, ffn_a=2 * (T - 2) + 1, next_a=2 * (T - 2) + 2,
                          misc_base=12 * (T - 1) - 1),
                Iteration(T, 0, cur=False, prep=False, ffn_a=2 * (T - 2) + 2,
                          next_a=2 * (T - 2) + 3, misc_base=12 * (T - 1) + 7)]
        LAST_FFN = 2 * T - 1
        assert (LOOP_TO - LOOP_FROM) % 2 == 0 and LOOP_FROM % 2 == 0

        def run(eng, steps):
            for it in head:
                steps(it)
            with eng.Fori(0, (LOOP_TO - LOOP_FROM) // 2) as pair:
                for r in range(2):
                    steps(full(pair * 2 + (LOOP_FROM + r), r))
            for it in tail:
                steps(it)

        CONSTS = 13
        PARAMS = 3 + 3 + 2 * 2 * LANES + 2 + 3
        SETD_SQUARES, SETD_BOUND, SETD_FIT, SETD_ALL = 2, 4, 9, 25

        def first_ffn(tile):
            return tile if isinstance(tile, int) and tile <= 3 else 2 * tile - 3

        def unit(u):
            return u // HALF, u // LANES % GROUPS, u % LANES

        def at_least(eng, s, n):
            if not isinstance(n, int) or n > 0:
                eng.wait_ge(s, n)

        block = ctx.enter_context(nc.Block())

        @block.sync
        def _(sp):
            def start_of(t):
                return t * (TILE * P) if isinstance(t, int) else sp.snap(t * (TILE * P))

            def tile_rows(flat, start):
                return flat[bass.ds(start, TILE * P)].rearrange("(b p a d) -> p b a d", b=2, p=P, a=2)

            def load_x(start):
                sp.dma_start(x0[:].rearrange("p (b a) d -> p b a d", b=2), tile_rows(x_flat, start)).then_inc(s_x0, 16)

            def store_x3(start):
                sp.dma_start(tile_rows(out_flat, start), x3[:].rearrange("p (b a) d -> p b a d", b=2)).then_inc(s_out, 16)

            def spread(par, lo, hi):
                n = 0
                for w, rows in ((0, q_rows), (1, k_rows)):
                    for part in range(PARTS):
                        src = (qk_lo if part == (2, 1)[w] else qk_hi)[w]
                        for j in range(LANES):
                            if lo <= n < hi:
                                sp.dma_start(rows[par][ROWS * j + HD * part:ROWS * j + HD * (part + 1), :, :],
                                             src[ROWS * j:ROWS * (j + 1), :]).then_inc(s_spread, 16)
                            n += 1

            def place_max(t, par, hb, use):
                sp.wait_ge(m_free, use + 1)
                at_least(sp, s_mrows, 64 * (4 * t + hb))
                b, g0 = hb // 2, 2 * (hb % 2)
                for j in range(LANES):
                    r = ROWS * j + HD * PARTS
                    sp.dma_start(q_rows[par][r:r + 2, g0:g0 + 2, b * SEQ:(b + 1) * SEQ],
                                 max_rows[4 * j:4 * j + 4, :]).then_inc(s_mrows, 16)

            perm = "(g j i) d -> j i g d"
            load_x(start_of(0))
            for dst, src in ((k0_raw, k0.rearrange("(c p) n -> p c n", p=P)),
                             (k1_raw, k1.rearrange("(c p) n -> p c n", p=P)),
                             (k2_raw, k2.rearrange("(c p) n -> p c n", p=P))):
                sp.dma_start(dst[:], src).then_inc(s_params, 16)
            for i, s in enumerate((s0, s1, s2)):
                sp.dma_start(s_raw[:, i:i + 1], s.partition_broadcast(P)).then_inc(s_params, 16)
            for i, (w, b) in enumerate(((wq, bq), (wk, bk), (wv, bv))):
                b2 = b.rearrange("(n a) -> n a", a=1)
                if i < 2:
                    for j in range(LANES):
                        rows = slice(ROWS * j, ROWS * (j + 1))
                        sp.dma_start(w_raw[rows, i, :], w.rearrange(perm, g=GROUPS, j=LANES)[j]).then_inc(s_params, 16)
                        with nc.allow_non_contiguous_dma(reason="128 biases"):
                            sp.dma_start(b_raw[rows, i:i + 1],
                                         b2.rearrange(perm, g=GROUPS, j=LANES)[j]).then_inc(s_params, 16)
                else:
                    sp.dma_start(w_raw[:, i, :], w).then_inc(s_params, 16)
                    sp.dma_start(b_raw[:, i:i + 1], b2).then_inc(s_params, 16)
            for dst, src in ((gamma_b, gamma), (beta_b, beta), (bv_b, bv)):
                sp.dma_start(dst[:], src.partition_broadcast(P)).then_inc(s_params, 16)
            sp.wait_ge(z_free, Z_USES)
            load_x(start_of(1))
            sp.wait_ge(m_free, 3)
            sp.wait_ge(s_const, CONSTS)
            spread(0, 0, SPREADS)

            def steps(it):
                t, par = it.t, it.par
                if it.ffn_b is not None:
                    start = start_of(t + 2)
                    sp.wait_ge(z_free, Z_USES * (first_ffn(t + 1) + 1))
                    load_x(start)
                if it.prev:
                    place_max(t - 1, 1 - par, 3, it.misc["MT3"])
                if it.cur:
                    place_max(t, par, 0, it.misc["MT0"])
                if it.ffn_a is not None:
                    start = start_of(t - 2)
                    sp.wait_ge(z_free, Z_USES * it.ffn_a + Z_USES)
                    store_x3(start)
                if it.prep:
                    sp.wait_ge(m_free, it.misc["K"] + 1)
                    if it.prev:
                        sp.wait_ge(t_full, UNITS * t + 1)
                    spread(1 - par, 0, 6)
                if it.cur:
                    place_max(t, par, 1, it.misc["MT1"])
                if it.prep:
                    spread(1 - par, 6, SPREADS)
                if it.cur:
                    place_max(t, par, 2, it.misc["MT2"])

            run(sp, steps)
            sp.wait_ge(z_free, Z_USES * (LAST_FFN + 1))
            store_x3(start_of(TILES - 1))
            sp.wait_ge(s_out, 16 * TILES)

        @block.gpsimd
        def _(pool):
            g = nc.gpsimd
            g.memset(ident[:], 0.0).then_inc(s_const, 1)
            g.memset(ident16[:], 0.0).then_inc(s_const, 1)
            pool.wait_ge(s_const, 2)
            for m in (ident, ident16):
                g.affine_select(out=m[:], in_=m[:], compare_op=ALU.not_equal, fill=1.0, base=0,
                                pattern=[[-1, P]], channel_multiplier=1).then_inc(s_const, 1)
            g.memset(minus_half[:], -0.5).then_inc(s_const, 1)
            g.memset(plus_half[:], 0.5).then_inc(s_const, 1)
            for i in range(2):
                g.memset(k_rows[i][:], -1.0 / M_UNIT).then_inc(s_const, 1)
                g.memset(v_cols[i][:], 0.0).then_inc(s_const, 1)
            g.memset(eps[:], EPS).then_inc(s_const, 1)
            pool.wait_ge(s_const, 11)
            for i in range(2):
                g.memset(v_cols[i][:, :, :, HD:HD + 1], 1.0).then_inc(s_const, 1)

            def normalize(dst, src, mv, xc, ve, rs, n, steps_done, k, done):
                shape = [P, n, P]
                g.tensor_tensor(ve[:], mv[:, :, 1], eps[:, 0:n], ALU.add).then_inc(steps_done, 1)
                g.tensor_tensor(xc[:], src, mv[:, :, 0:1].broadcast_to(shape), ALU.subtract)
                pool.wait_ge(steps_done, k + 1)
                g.tensor_tensor(rs[:], ve[:], minus_half[:, 0:n], ALU.pow).then_inc(steps_done, 1)
                pool.wait_ge(steps_done, k + 2)
                g.tensor_tensor(dst, xc[:], rs[:].unsqueeze(2).broadcast_to(shape), ALU.mult).then_inc(done, 1)

            def ffn_norm(f, src):
                at_least(pool, z_full, Z_USES * f - (Z_USES - 1))
                pool.wait_ge(f_mv, f + 1)
                normalize(ffn_xn[:], src[:], ffn_mv, ffn_xc, ffn_ve, ffn_rs, TT, f_rs, 2 * f, f_xn)

            def att_norm(t, par):
                pool.wait_ge(a_mv, t + 1)
                normalize(att_xn[par][:], x1[par][:], att_mv, att_xc, att_ve, att_rs, TT, a_rs, 2 * t, a_xn)

            def tail_y(t, b, use):
                pool.wait_ge(s_base, t + 1)
                pool.wait_ge(m_free, use + 1)
                g.tensor_tensor(att_y[:], ctx_n[:], xn_bv[:, 2 * b:2 * b + 2, :], ALU.add).then_inc(s_y, 1)

            def tail_norm(t, b, par):
                n = 2 * t + b
                pool.wait_ge(t_mv, n + 1)
                normalize(tail_n[:], att_y[:], tail_mv, tail_xc, tail_ve, tail_rs, 2, t_rs, 2 * n, t_n)
                pool.wait_ge(t_n, 2 * n + 1)
                g.tensor_tensor(tail_g[:], tail_n[:], gamma_b[:].unsqueeze(1).broadcast_to([P, 2, P]),
                                ALU.mult).then_inc(t_n, 1)
                pool.wait_ge(t_n, 2 * n + 2)
                g.tensor_tensor(x2[par][:, 2 * b:2 * b + 2, :], tail_g[:], x1_beta[:, 2 * b:2 * b + 2, :],
                                ALU.add).then_inc(s_x2, 1)

            def tail_base(t, par):
                at_least(pool, s_x2, 2 * t)
                g.tensor_tensor(x1_beta[:], x1[par][:], beta_b[:].unsqueeze(1).broadcast_to([P, TT, P]), ALU.add)
                g.tensor_tensor(xn_bv[:], att_xn[par][:], bv_b[:].unsqueeze(1).broadcast_to([P, TT, P]),
                                ALU.add).then_inc(s_base, 1)

            pool.wait_ge(s_setd, SETD_SQUARES)
            g.tensor_tensor(w_norm[:], w_bound[:], plus_half[:], ALU.pow).then_inc(s_setp, 1)
            pool.wait_ge(s_setd, SETD_BOUND)
            g.partition_all_reduce(w_most[:], w_inv[:], P, RMAX).then_inc(s_setp, 1)
            ffn_norm(0, x0)
            pool.wait_ge(s_params, 16 * PARAMS)
            att_norm(0, 0)
            ffn_norm(1, x0)

            def steps(it):
                t, par = it.t, it.par
                if it.prep:
                    att_norm(t + 1, 1 - par)
                if it.prev:
                    tail_y(t - 1, 0, it.misc["CT01"])
                    tail_norm(t - 1, 0, 1 - par)
                if it.ffn_b is not None:
                    ffn_norm(it.ffn_b, x0)
                if it.prev:
                    tail_y(t - 1, 1, it.misc["CT11"])
                    tail_norm(t - 1, 1, 1 - par)
                if it.cur:
                    tail_base(t, par)
                if it.next_a is not None:
                    ffn_norm(it.next_a, x2[1 - par])

            run(pool, steps)

        @block.tensor
        def _(pe):
            def bank_of(use):
                return ps_z[use % 2]

            def ffn_transpose(f):
                at_least(pe, z_free, Z_USES * f - 1)
                pe.wait_ge(f_xn, f + 1)
                for i in range(TT):
                    last = pe.transpose(bank_of(0)[:, i * P:(i + 1) * P], ffn_xn[:, i, :], ident[:])
                last.then_inc(z_full, 1)

            def ffn_in(f, m):
                pe.wait_ge(z_free, Z_USES * f + 1 + max(0, m - 1))
                o = bank_of(1 + m)
                pe.matmul(o[:], w0[:, m * P:(m + 1) * P], ffn_hi[:, 0, :], start=True, stop=False)
                pe.matmul(o[:], w0[:, m * P:(m + 1) * P], ffn_lo[:, 0, :], start=False, stop=True).then_inc(z_full, 1)

            def ffn_mid(f, m, half):
                o = bank_of(5 + m)
                for k in (0, 1) if half == 0 else (2, 3):
                    pe.wait_ge(z_free, Z_USES * f + max(2 + k, 4 + m))
                    w = w1[:, k, m * P:(m + 1) * P]
                    pe.matmul(o[:], w, ffn_hi[:, 1 + k, :], start=(k == 0), stop=False)
                    last = pe.matmul(o[:], w, ffn_lo[:, 1 + k, :], start=False, stop=(k == KC - 1))
                if half:
                    last.then_inc(z_full, 1)

            def ffn_out(f, i):
                o = bank_of(9)[:, i * P:(i + 1) * P]
                for k in range(KC):
                    if i == 0:
                        pe.wait_ge(z_free, Z_USES * f + max(6 + k, 8))
                    pe.matmul(o, ffn_hi[:, 5 + k, i * P:(i + 1) * P], w2[:, k, :], start=(k == 0), stop=False)
                    last = pe.matmul(o, ffn_lo[:, 5 + k, i * P:(i + 1) * P], w2[:, k, :], start=False,
                                     stop=(k == KC - 1))
                if i == TT - 1:
                    last.then_inc(z_full, 1)

            def ffn_piece(f, s):
                if s == 0:
                    pass
                elif s == 1:
                    ffn_transpose(f)
                elif s == 2:
                    ffn_in(f, 0)
                    ffn_in(f, 1)
                elif s == 3:
                    ffn_in(f, 2)
                    ffn_in(f, 3)
                elif s < 12:
                    ffn_mid(f, (s - 4) // 2, s % 2)
                else:
                    ffn_out(f, s - 12)

            def misc_wait(use):
                at_least(pe, m_free, use)

            def att_transpose(t, par, use):
                misc_wait(use)
                pe.wait_ge(a_xn, t + 1)
                for i in range(TT):
                    last = pe.transpose(ps_m[:, i * P:(i + 1) * P], att_xn[par][:, i, :], ident[:])
                last.then_inc(m_full, 1)

            def project(w, use):
                misc_wait(use)
                n = 0
                for ww in (wt_hi, wt_lo):
                    for xx in (att_hi, att_lo):
                        last = pe.matmul(ps_m[:], ww[:, w, :], xx[:], start=(n == 0), stop=(n == 3))
                        n += 1
                last.then_inc(m_full, 1)

            def project_v(use):
                misc_wait(use)
                for i in range(TT):
                    n = 0
                    for xx in (att_hi, att_lo):
                        for ww in (wt_hi, wt_lo):
                            last = pe.matmul(ps_m[:, i * P:(i + 1) * P], xx[:, i * P:(i + 1) * P], ww[:, 2, :],
                                             start=(n == 0), stop=(n == 3))
                            n += 1
                last.then_inc(m_full, 1)

            def scores(t, par, u):
                b, g, j = unit(u)
                n = UNITS * t + u
                if u == 0:
                    pe.wait_ge(s_spread, 16 * SPREADS * (t + 1))
                at_least(pe, s_max, n - 1)
                r = slice(ROWS * j, ROWS * j + HD * PARTS)
                for a in range(2):
                    c = b * SEQ + a * P
                    last = pe.matmul(ps_s[u % 2][:, a * SEQ:(a + 1) * SEQ], q_rows[par][r, g, c:c + P],
                                     k_rows[par][r, g, b * SEQ:(b + 1) * SEQ], start=True, stop=True)
                last.then_inc(s_full, 1)

            def shifted(t, par, u):
                b, g, j = unit(u)
                n = UNITS * t + u
                if u % HB == 0:
                    pe.wait_ge(s_mrows, 64 * (4 * t + u // HB + 1))
                at_least(pe, s_exp, n - 1)
                r = slice(ROWS * j, ROWS * j + HD * PARTS + 2)
                for a in range(2):
                    c = b * SEQ + a * P
                    last = pe.matmul(ps_t[u % 2][:, a * SEQ:(a + 1) * SEQ], k_rows[par][r, g, c:c + P],
                                     q_rows[par][r, g, b * SEQ:(b + 1) * SEQ], start=True, stop=True)
                last.then_inc(t_full, 1)

            def context(t, par, grp):
                b, g = grp // GROUPS, grp % GROUPS
                n = 2 * GROUPS * t + grp
                pe.wait_ge(s_exp, LANES * n + LANES)
                at_least(pe, c_free, n)
                for a in range(2):
                    for j in range(LANES):
                        last = pe.matmul(ps_c[ROWS * j:ROWS * (j + 1), 0:SEQ], v_cols[par][:, 2 * b + a, LANES * g + j, :],
                                         probs[grp % 2][:, j, a * SEQ:(a + 1) * SEQ], start=(a == 0), stop=(a == 1))
                last.then_inc(c_full, 1)

            def context_transpose(t, b, a, use):
                misc_wait(use)
                pe.wait_ge(c_free, 2 * GROUPS * t + GROUPS * (b + 1))
                for g in range(GROUPS):
                    last = pe.transpose(ps_m[:, g * P:(g + 1) * P], ctx_t[:, g, a * P:(a + 1) * P], ident[:])
                last.then_inc(m_full, 1)

            def max_transpose(t, hb, use):
                misc_wait(use)
                pe.wait_ge(s_mparts, 2 * (4 * t + hb + 1))
                for a in range(2):
                    last = pe.transpose(ps_m[:].bitcast(F16)[0:4 * LANES, a * P:(a + 1) * P],
                                        max_parts[:, a * LANES:(a + 1) * LANES].rearrange("p j c g -> p (j c g)"),
                                        ident16[:])
                last.then_inc(m_full, 1)

            pe.wait_ge(s_const, CONSTS)
            pe.wait_ge(s_setd, SETD_FIT)
            for i in range(3):
                last = pe.transpose(ps_c[:, i * P:(i + 1) * P], w_fit[:, i, :], ident[:])
            last.then_inc(s_wt, 1)
            pe.wait_ge(s_setd, SETD_ALL)
            for s in range(16):
                ffn_piece(0, s)
            att_transpose(0, 0, 0)
            project(0, 1)
            project(1, 2)
            project_v(3)
            for s in range(16):
                ffn_piece(1, s)

            def steps(it):
                t, par = it.t, it.par
                for s in range(UNITS):
                    if it.cur:
                        scores(t, par, s)
                    if s < HALF:
                        if it.prev:
                            shifted(t - 1, 1 - par, s + HALF)
                    elif it.cur:
                        shifted(t, par, s - HALF)
                    if s < HALF and it.ffn_a is not None:
                        ffn_piece(it.ffn_a, s)
                    if s >= HALF and it.ffn_b is not None:
                        ffn_piece(it.ffn_b, s - HALF)
                    if it.prev:
                        if s in (1, 5, 9, 13, 17):
                            context(t - 1, 1 - par, s // 4 + 3)
                        if s == 1:
                            max_transpose(t - 1, 3, it.misc["MT3"])
                        for b, first in ((0, 3), (1, 19)):
                            if s in (first, first + 1):
                                a = s - first
                                context_transpose(t - 1, b, a, it.misc[f"CT{b}{a}"])
                    if it.cur:
                        if s in (21, 25, 29):
                            context(t, par, (s - 21) // 4)
                        if s in (9, 17, 25):
                            max_transpose(t, s // 8 - 1, it.misc[f"MT{s // 8 - 1}"])
                    if it.prep:
                        if s == AT_LNT:
                            att_transpose(t + 1, 1 - par, it.misc["LNT"])
                        if s == AT_Q:
                            project(0, it.misc["Q"])
                        if s == AT_K:
                            project(1, it.misc["K"])
                        if s == AT_V:
                            project_v(it.misc["V"])

            run(pe, steps)
            for s in range(16):
                ffn_piece(LAST_FFN, s)

        @block.scalar
        def _(act):
            a_ = nc.scalar

            def z_split(f, use):
                act.wait_ge(z_full, Z_USES * f + use + 1)
                a_.activation(ffn_hi[:, use, :], ps_z[use % 2][:], ACT.Relu if use else ACT.Copy,
                              scale=1.0 if use else XN_SCALE).then_inc(z_hi, 1)

            def ffn_piece(f, s):
                if s in (1, 5, 7, 9, 11):
                    z_split(f, {1: 0, 5: 5, 7: 6, 9: 7, 11: 8}[s])
                elif s in (2, 3):
                    z_split(f, 2 * s - 3)
                    z_split(f, 2 * s - 2)

            def att_split(use):
                act.wait_ge(m_full, use + 1)
                a_.activation(att_hi[:], ps_m[:], ACT.Copy, scale=XN_SCALE).then_inc(m_hi, 1)

            def qk_split(w, use):
                act.wait_ge(m_full, use + 1)
                a_.activation(qk_hi[w][:], ps_m[:], ACT.Identity, bias=b_fit[:, w:w + 1]).then_inc(m_hi, 1)

            def v_copy(t, par, use):
                act.wait_ge(m_full, use + 1)
                at_least(act, c_full, 2 * GROUPS * (t - 1))
                a_.activation(v_cols[par][:].rearrange("p t h r -> p (t h) r")[:, :, 0:HD],
                              ps_m[:].rearrange("p (n i) -> p n i", i=HD), ACT.Copy,
                              scale=v_unscale[:, 0:1]).then_inc(m_free, 1)

            def exps(t, u):
                n = UNITS * t + u
                grp = u // LANES
                act.wait_ge(t_full, n + 1)
                if u % LANES == 0:
                    at_least(act, c_full, 2 * GROUPS * t + grp - 1)
                a_.activation(probs[grp % 2][:, u % LANES, :], ps_t[u % 2][:], ACT.Exp,
                              scale=score_scale[:, 0:1]).then_inc(s_exp, 1)

            def context_copy(t, grp):
                act.wait_ge(c_full, 2 * GROUPS * t + grp + 1)
                a_.activation(ctx_t[:, grp % GROUPS, :], ps_c[:, 0:SEQ], ACT.Copy).then_inc(c_free, 1)

            act.wait_ge(s_wt, 1)
            a_.activation(wt_hi[:].rearrange("p i n -> p (i n)"), ps_c[:, 0:3 * P], ACT.Copy).then_inc(s_wthi, 1)
            act.wait_ge(s_setd, SETD_ALL)
            for s in range(16):
                ffn_piece(0, s)
            att_split(0)
            qk_split(0, 1)
            qk_split(1, 2)
            act.wait_ge(s_const, CONSTS)
            v_copy(0, 0, 3)
            for s in range(16):
                ffn_piece(1, s)

            def steps(it):
                t, par = it.t, it.par
                for s in range(UNITS):
                    if s < HALF:
                        if it.prev:
                            exps(t - 1, s + HALF)
                    elif it.cur:
                        exps(t, s - HALF)
                    if s < HALF and it.ffn_a is not None:
                        ffn_piece(it.ffn_a, s)
                    if s >= HALF and it.ffn_b is not None:
                        ffn_piece(it.ffn_b, s - HALF)
                    if it.prev and s in (1, 5, 9, 13, 17):
                        context_copy(t - 1, s // 4 + 3)
                    if it.cur and s in (21, 25, 29):
                        context_copy(t, (s - 21) // 4)
                    if it.prep:
                        if s == AT_LNT:
                            att_split(it.misc["LNT"])
                        if s == AT_Q:
                            qk_split(0, it.misc["Q"])
                        if s == AT_K:
                            qk_split(1, it.misc["K"])
                        if s == AT_V:
                            v_copy(t + 1, 1 - par, it.misc["V"])

            run(act, steps)
            for s in range(16):
                ffn_piece(LAST_FFN, s)

        @block.vector
        def _(dve):
            v = nc.vector
            done = [0]

            def step(ins):
                done[0] += 1
                ins.then_inc(s_setd, 1)

            def so_far():
                dve.wait_ge(s_setd, done[0])

            dve.wait_ge(s_params, 16 * PARAMS)
            step(v.tensor_tensor(w_sq[:], w_raw[:], w_raw[:], ALU.mult))
            so_far()
            step(v.tensor_reduce(w_bound[:], w_sq[:], AX.X, ALU.add))
            assert done[0] == SETD_SQUARES
            step(v.scalar_tensor_tensor(out=b_abs[:], in0=b_raw[:], scalar=-1.0, in1=b_raw[:], op0=ALU.mult, op1=ALU.max))
            so_far()
            dve.wait_ge(s_setp, 1)
            step(v.scalar_tensor_tensor(out=w_inv[:], in0=w_norm[:], scalar=float(P) ** 0.5, in1=b_abs[:],
                                        op0=ALU.mult, op1=ALU.add))
            assert done[0] == SETD_BOUND
            dve.wait_ge(s_setp, 2)
            step(v.tensor_scalar(w_norm[:], w_most[:], 1e-30, None, ALU.max))
            so_far()
            step(v.reciprocal(w_inv[:], w_norm[:]))
            so_far()
            step(v.tensor_scalar(w_factor[:], w_inv[:], Q_MAX, None, ALU.mult))
            so_far()
            step(v.tensor_tensor(b_fit[:], b_raw[:], w_factor[:], ALU.mult))
            for i in range(3):
                last = v.tensor_scalar(w_fit[:, i, :], w_raw[:, i, :], w_factor[:, i:i + 1], 1.0 / XN_SCALE,
                                       ALU.mult, ALU.mult)
            step(last)
            assert done[0] == SETD_FIT
            step(v.tensor_scalar(score_tmp[:], w_norm[:, 0:1], w_norm[:, 1:2], Q_MAX ** -2, ALU.mult, ALU.mult))
            so_far()
            step(v.tensor_scalar(score_scale[:], score_tmp[:], float(1.0 / np.sqrt(HD)), None, ALU.mult))
            step(v.tensor_scalar(v_unscale[:], w_norm[:, 2:3], 1.0 / Q_MAX, None, ALU.mult))
            step(v.tensor_scalar(s_tmp[:, 0:2], s_raw[:, 0:2], 0.0, None, ALU.is_ge))
            so_far()
            step(v.tensor_scalar(s_sign[:], s_tmp[:, 0:2], 2.0, -1.0, ALU.mult, ALU.add))
            so_far()
            step(v.tensor_scalar(w0_scale[:], s_sign[:, 0:1], W0_UNIT, None, ALU.mult))
            step(v.tensor_scalar(w1_scale[:, 0:1], s_sign[:, 1:2], 2 * W1_UNIT, None, ALU.mult))
            step(v.tensor_scalar(w1_scale[:, 1:2], s_sign[:, 1:2], W1_UNIT, None, ALU.mult))
            step(v.tensor_tensor(s_tmp[:, 2:4], s_raw[:, 0:2], s_sign[:], ALU.mult))
            step(v.tensor_tensor(w0_diff[:], k0_raw[:, 0, :], k0_raw[:, 1, :], ALU.subtract))
            so_far()
            step(v.tensor_scalar(score_tmp[:], s_tmp[:, 2:3], s_tmp[:, 3:4], FFN_OUT, ALU.mult, ALU.mult))
            so_far()
            step(v.tensor_tensor(ffn_scale[:], score_tmp[:], s_raw[:, 2:3], ALU.mult))
            step(v.tensor_scalar(w0[:], w0_diff[:], w0_scale[:, 0:1], None, ALU.mult))
            step(v.tensor_scalar(w1[:], k1_raw[:], w1_scale[:, 0:1], w1_scale[:, 1:2], ALU.mult, ALU.subtract))
            step(v.tensor_scalar(w2[:], k2_raw[:], 2.0, -1.0, ALU.mult, ALU.add))
            dve.wait_ge(s_wthi, 1)
            step(v.tensor_tensor(wt_lo[:].rearrange("p i n -> p (i n)"), ps_c[:, 0:3 * P],
                                 wt_hi[:].rearrange("p i n -> p (i n)"), ALU.subtract))
            assert done[0] == SETD_ALL
            so_far()

            def stats(src, bn, n, bn_done):
                for i in range(n):
                    last = v.bn_stats(bn[:, i, :], src[:, i, :])
                last.then_inc(bn_done, 1)

            def mean_var(bn, mv, n, mv_done):
                for i in range(n):
                    last = v.bn_aggr(mv[:, i, :], bn[:, i, :])
                last.then_inc(mv_done, 1)

            def ffn_stats(src):
                stats(src, ffn_bn, TT, f_bn)

            def ffn_mean_var(f):
                mean_var(ffn_bn, ffn_mv, TT, f_mv)

            def ffn_mean_var_wait(f):
                at_least(dve, f_xn, f)
                dve.wait_ge(f_bn, f + 1)

            def z_rest(f, use):
                dve.wait_ge(z_hi, 9 * f + use + 1)
                if use:
                    v.scalar_tensor_tensor(out=ffn_lo[:, use, :], in0=ps_z[use % 2][:], scalar=0.0,
                                           in1=ffn_hi[:, use, :], op0=ALU.max, op1=ALU.subtract).then_inc(z_free, 1)
                else:
                    v.scalar_tensor_tensor(out=ffn_lo[:, 0, :], in0=ps_z[0][:], scalar=XN_SCALE,
                                           in1=ffn_hi[:, 0, :], op0=ALU.mult, op1=ALU.subtract).then_inc(z_free, 1)

            def ffn_residual(f, src, dst, stored=None, based=None):
                dve.wait_ge(z_full, Z_USES * f + Z_USES)
                if based is not None:
                    dve.wait_ge(s_base, based)
                if stored is not None:
                    at_least(dve, s_out, 16 * stored)
                v.scalar_tensor_tensor(out=dst[:].rearrange("p t d -> p (t d)"), in0=ps_z[1][:],
                                       scalar=ffn_scale[:, 0:1], in1=src[:].rearrange("p t d -> p (t d)"),
                                       op0=ALU.mult, op1=ALU.add).then_inc(z_free, 1)

            def ffn_piece(f, s, src, dst, stored=None, based=None):
                if s in (1, 5, 7, 9, 11):
                    z_rest(f, {1: 0, 5: 5, 7: 6, 9: 7, 11: 8}[s])
                elif s in (2, 3):
                    z_rest(f, 2 * s - 3)
                    z_rest(f, 2 * s - 2)
                elif s == 15:
                    ffn_residual(f, src, dst, stored, based)

            def att_stats(par, f):
                dve.wait_ge(z_free, Z_USES * (f + 1))
                stats(x1[par], att_bn, TT, a_bn)

            def att_mean_var_wait(t):
                at_least(dve, a_xn, t)
                dve.wait_ge(a_bn, t + 1)

            def att_rest(t):
                dve.wait_ge(m_hi, 3 * t + 1)
                v.scalar_tensor_tensor(out=att_lo[:], in0=ps_m[:], scalar=XN_SCALE, in1=att_hi[:],
                                       op0=ALU.mult, op1=ALU.subtract).then_inc(m_free, 1)

            def qk_rest(t, w):
                dve.wait_ge(m_hi, 3 * t + 2 + w)
                v.scalar_tensor_tensor(out=qk_lo[w][:], in0=ps_m[:], scalar=b_fit[:, w:w + 1], in1=qk_hi[w][:],
                                       op0=ALU.add, op1=ALU.subtract).then_inc(m_free, 1)

            def row_maxima(t, u):
                b, g, j = unit(u)
                dve.wait_ge(s_full, UNITS * t + u + 1)
                if u % HB == 0:
                    at_least(dve, s_mparts, 2 * (4 * t + u // HB))
                v.tensor_reduce(row_max[:, j::LANES, g % 2],
                                ps_s[u % 2][:].rearrange("p (a k) -> p a k", a=2), AX.X, ALU.max).then_inc(s_max, 1)

            def split_max(t, hb):
                n = 4 * t + hb
                dve.wait_ge(s_max, UNITS * t + HB * (hb + 1))
                v.tensor_scalar(max_parts[:, :, 0, :], row_max[:], M_UNIT, None, ALU.mult).then_inc(s_mparts, 1)
                dve.wait_ge(s_mparts, 2 * n + 1)
                v.scalar_tensor_tensor(out=max_parts[:, :, 1, :], in0=row_max[:], scalar=M_UNIT,
                                       in1=max_parts[:, :, 0, :], op0=ALU.mult, op1=ALU.subtract).then_inc(s_mparts, 1)

            def copy_max(t, hb, use):
                dve.wait_ge(m_full, use + 1)
                at_least(dve, s_mrows, 64 * (4 * t + hb))
                v.tensor_copy(max_rows[:], ps_m[:].bitcast(F16)[0:4 * LANES, 0:SEQ]).then_inc(m_free, 1)

            def context_norm(t, b, a, use):
                n = 4 * t + 2 * b + a
                dve.wait_ge(m_full, use + 1)
                c = ps_m[:].rearrange("p (h r) -> p h r", r=ROWS)
                v.reciprocal(den[:], c[:, :, HD]).then_inc(s_den, 1)
                dve.wait_ge(s_den, n + 1)
                at_least(dve, s_y, 2 * t + b)
                v.tensor_tensor(ctx_n[:, a, :].rearrange("p (h i) -> p h i", i=HD), c[:, :, 0:HD],
                                den[:].unsqueeze(2).broadcast_to([P, HEADS, HD]), ALU.mult).then_inc(m_free, 1)

            def tail_stats(t, b):
                dve.wait_ge(s_y, 2 * t + b + 1)
                stats(att_y, tail_bn, 2, t_bn)

            dve.wait_ge(s_x0, 16)
            ffn_stats(x0)
            ffn_mean_var_wait(0)
            ffn_mean_var(0)
            for s in range(16):
                ffn_piece(0, s, x0, x1[0])
            att_stats(0, 0)
            att_mean_var_wait(0)
            mean_var(att_bn, att_mv, TT, a_mv)
            dve.wait_ge(s_x0, 32)
            ffn_stats(x0)
            ffn_mean_var_wait(1)
            ffn_mean_var(1)
            att_rest(0)
            qk_rest(0, 0)
            qk_rest(0, 1)
            for s in range(16):
                ffn_piece(1, s, x0, x1[1])

            def steps(it):
                t, par = it.t, it.par
                for s in range(UNITS):
                    norm_prep = it.prep and s == AT_STATS_PREP + 1
                    norm_b = it.ffn_b is not None and s == AT_STATS_B + 1
                    norm_a = it.next_a is not None and s == AT_STATS_A + 1
                    norm_tail = it.prev and s in (8, 24)
                    if norm_prep:
                        att_mean_var_wait(t + 1)
                    if norm_b:
                        ffn_mean_var_wait(it.ffn_b)
                    if norm_a:
                        ffn_mean_var_wait(it.next_a)
                    if norm_tail:
                        dve.wait_ge(t_bn, 2 * (t - 1) + s // HALF + 1)
                    if it.cur:
                        row_maxima(t, s)
                    if norm_prep:
                        mean_var(att_bn, att_mv, TT, a_mv)
                    if norm_b:
                        ffn_mean_var(it.ffn_b)
                    if norm_a:
                        ffn_mean_var(it.next_a)
                    if norm_tail:
                        mean_var(tail_bn, tail_mv, 2, t_mv)
                    if it.cur and s % HB == HB - 1:
                        split_max(t, s // HB)
                    if s < HALF and it.ffn_a is not None:
                        ffn_piece(it.ffn_a, s, x2[par], x3, stored=t - 2)
                    if s >= HALF and it.ffn_b is not None:
                        ffn_piece(it.ffn_b, s - HALF, x0, x1[par], based=t + 1)
                    if it.prev:
                        if s == 1:
                            copy_max(t - 1, 3, it.misc["MT3"])
                        for b, first in ((0, 3), (1, 19)):
                            if s in (first, first + 1):
                                a = s - first
                                context_norm(t - 1, b, a, it.misc[f"CT{b}{a}"])
                            if s == first + 4:
                                tail_stats(t - 1, b)
                    if it.cur and s in (9, 17, 25):
                        copy_max(t, s // 8 - 1, it.misc[f"MT{s // 8 - 1}"])
                    if it.prep:
                        if s == AT_STATS_PREP:
                            att_stats(1 - par, first_ffn(t + 1))
                        if s == AT_LNT:
                            att_rest(t + 1)
                        if s == AT_Q:
                            qk_rest(t + 1, 0)
                        if s == AT_K:
                            qk_rest(t + 1, 1)
                    if it.ffn_b is not None and s == AT_STATS_B:
                        dve.wait_ge(s_x0, 16 * (t + 3))
                        ffn_stats(x0)
                    if it.next_a is not None and s == AT_STATS_A:
                        dve.wait_ge(s_x2, 2 * t)
                        ffn_stats(x2[1 - par])

            run(dve, steps)
            for s in range(16):
                ffn_piece(LAST_FFN, s, x2[(TILES - 1) % 2], x3, stored=TILES - 1)


NAMES = ["L0_attn_x", "L0_attn_Wq", "L0_attn_bq", "L0_attn_Wk", "L0_attn_bk", "L0_attn_Wv", "L0_attn_bv",
         "L0_attn_gamma", "L0_attn_beta", "L0_ffn_k0", "L0_ffn_k1", "L0_ffn_k2", "L0_ffn_s0", "L0_ffn_s1", "L0_ffn_s2"]


def kernel(**inputs):
    import concourse.bacc as bacc
    from concourse.bass_utils import run_bass_kernel_spmd

    nc = bacc.Bacc("TRN2", target_bir_lowering=False, num_devices=1)
    arrays, args = {}, []
    for name in NAMES:
        a = np.ascontiguousarray(inputs[name])
        if a.ndim == 0:
            a = a.reshape(1)
        arrays[name] = a
        args.append(nc.dram_tensor(name, a.shape, mybir.dt.from_np(a.dtype), kind="ExternalInput").ap())
    shape = inputs["L0_attn_x"].shape
    args.append(nc.dram_tensor("y", shape, F32, kind="ExternalOutput").ap())
    macaron_layer(nc, *args)
    result = run_bass_kernel_spmd(nc, [arrays], core_ids=[0])
    return result.results[0]["y"]
```

```python
import numpy as np
from contextlib import ExitStack

import concourse.bass as bass
from concourse import mybir
from concourse.alu_op_type import AluOpType as ALU

F32 = mybir.dt.float32
F16 = mybir.dt.float16
U8 = mybir.dt.uint8
ACT = mybir.ActivationFunctionType
AX = mybir.AxisListType
RMAX = bass.bass_isa.ReduceOp.max

P = 128
SEQ = 256
TILE = 512
TT = TILE // P
HEADS, HD = 16, 8
GROUPS, LANES = 4, 4
ROWS = 32
PARTS = 3
UNITS = 32
HALF = 16
HB = 8
HIDDEN = 512
KC = HIDDEN // P
EPS = 1e-5
XN_SCALE = 2.0 ** 8
W0_UNIT = 0.5
W1_UNIT = 2.0 ** -8
Q_MAX = 2.0 ** 13
M_UNIT = 2.0 ** -14
FFN_OUT = 0.5 * 2 * 2 / (XN_SCALE * W0_UNIT / 2 * W1_UNIT)

MISC = [("CT00", 4), ("CT01", 6), ("LNT", 9), ("Q", 10), ("K", 13), ("V", 17), ("CT10", 18), ("CT11", 20)]
AT = dict(MISC)
AT_MAX = (10, 18, 26, 2)
PREP_USES = ("LNT", "Q", "K", "V")
Z_USES = 10
SPREADS = 2 * LANES * PARTS
AT_STATS_PREP, AT_STATS_B, AT_STATS_A = 6, 6, 26
AT_STATS_TAIL = (12, 22)

FFN_IN = {2: 0, 3: 1, 4: 2, 5: 3}
FFN_MID = ((6, 0, 2), (7, 2, 5), (8, 5, 8), (9, 8, 11), (10, 11, 14), (11, 14, 16))
FFN_MID_DONE = {7: 0, 8: 1, 10: 2, 11: 3}
FFN_RESIDUAL = 14


class Iteration:

    def __init__(self, t, par, cur=True, prev=True, prep=True, ffn_a=None, ffn_b=None,
                 next_a=None, misc_base=None, load=True):
        self.t, self.par, self.cur, self.prev, self.prep = t, par, cur, prev, prep
        self.ffn_a, self.ffn_b = ffn_a, ffn_b
        self.load = load
        self.next_a = next_a
        names = [n for n, _ in MISC if
                 (n in PREP_USES and prep) or (n in ("CT00", "CT01", "CT10", "CT11") and prev)]
        self.misc = {n: misc_base + i for i, n in enumerate(names)}


def macaron_layer(nc, x, wq, bq, wk, bk, wv, bv, gamma, beta, k0, k1, k2, s0, s1, s2, out):
    tokens = x.shape[0] * x.shape[1]
    TILES = tokens // TILE
    x_flat = x.rearrange("n s d -> (n s d)")
    out_flat = out.rearrange("n s d -> (n s d)")

    with ExitStack() as ctx:
        def sb(name, shape, dt=F32):
            return ctx.enter_context(nc.sbuf_tensor(name, shape, dt))

        def bank(name):
            return ctx.enter_context(nc.psum_tensor(name, [P, TILE], F32))

        def sem(name):
            return ctx.enter_context(nc.semaphore(name))

        ident = sb("ident", [P, P])
        ident16 = sb("ident16", [P, P], F16)
        lane_order = sb("lane_order", [P, P])
        k0_raw = sb("k0_raw", [P, 2, HIDDEN], U8)
        k1_raw = sb("k1_raw", [P, KC, HIDDEN], U8)
        k2_raw = sb("k2_raw", [P, KC, P], U8)
        w0 = sb("w0", [P, HIDDEN], F16)
        w0_diff = sb("w0_diff", [P, HIDDEN], F16)
        w1 = sb("w1", [P, KC, HIDDEN], F16)
        w2 = sb("w2", [P, KC, P], F16)
        s_raw = sb("s_raw", [P, 3])
        s_sign = sb("s_sign", [P, 2])
        s_tmp = sb("s_tmp", [P, 4])
        w0_scale = sb("w0_scale", [P, 1])
        w1_scale = sb("w1_scale", [P, 2])
        ffn_scale = sb("ffn_scale", [P, 1])
        w_raw = sb("w_raw", [P, 3, P])
        w_sq = sb("w_sq", [P, 3, P])
        w_fit = sb("w_fit", [P, 3, P])
        b_raw = sb("b_raw", [P, 3])
        b_abs = sb("b_abs", [P, 3])
        b_fit = sb("b_fit", [P, 3])
        w_norm = sb("w_norm", [P, 3])
        w_bound = sb("w_bound", [P, 3])
        w_most = sb("w_most", [P, 3])
        w_inv = sb("w_inv", [P, 3])
        w_factor = sb("w_factor", [P, 3])
        score_tmp = sb("score_tmp", [P, 1])
        score_scale = sb("score_scale", [P, 1])
        v_unscale = sb("v_unscale", [P, 1])
        wt_hi = sb("wt_hi", [P, 3, P], F16)
        wt_lo = sb("wt_lo", [P, 3, P], F16)
        gamma_b = sb("gamma_b", [P, P])
        beta_b = sb("beta_b", [P, P])
        bv_b = sb("bv_b", [P, P])
        minus_half = sb("minus_half", [P, TT])
        plus_half = sb("plus_half", [P, 3])
        eps = sb("eps", [P, TT])
        x0 = sb("x0", [P, TT, P])
        x1 = [sb(f"x1_{i}", [P, TT, P]) for i in range(2)]
        x2 = [sb(f"x2_{i}", [P, TT, P]) for i in range(2)]
        x3 = sb("x3", [P, TT, P])
        ffn_bn = sb("ffn_bn", [P, TT, 6])
        ffn_mv = sb("ffn_mv", [P, TT, 2])
        ffn_xc = sb("ffn_xc", [P, TT, P])
        ffn_ve = sb("ffn_ve", [P, TT])
        ffn_rs = sb("ffn_rs", [P, TT])
        ffn_xn = sb("ffn_xn", [P, TT, P])
        ffn_hi = sb("ffn_hi", [P, 9, TILE], F16)
        ffn_lo = sb("ffn_lo", [P, 9, TILE], F16)
        att_bn = sb("att_bn", [P, TT, 6])
        att_mv = sb("att_mv", [P, TT, 2])
        att_xc = sb("att_xc", [P, TT, P])
        att_ve = sb("att_ve", [P, TT])
        att_rs = sb("att_rs", [P, TT])
        att_xn = [sb(f"att_xn{i}", [P, TT, P]) for i in range(2)]
        att_hi = sb("att_hi", [P, TILE], F16)
        att_lo = sb("att_lo", [P, TILE], F16)
        qk_hi = [sb(f"{n}_hi", [P, TILE], F16) for n in "qk"]
        qk_lo = [sb(f"{n}_lo", [P, TILE], F16) for n in "qk"]
        q_rows = [sb(f"q_rows{i}", [P, GROUPS, TILE], F16) for i in range(2)]
        k_rows = [sb(f"k_rows{i}", [P, GROUPS, TILE], F16) for i in range(2)]
        v_cols = [sb(f"v_cols{i}", [P, TT, HEADS, ROWS]) for i in range(2)]
        row_max = sb("row_max", [P, 2 * LANES, 2])
        max_parts = sb("max_parts", [P, 2 * LANES, 2, 2], F16)
        max_rows = sb("max_rows", [4 * LANES, SEQ], F16)
        probs = [sb(f"probs{i}", [P, LANES, TILE]) for i in range(2)]
        ctx_t = sb("ctx_t", [P, 2 * GROUPS, SEQ])
        den = sb("den", [P, HEADS])
        ctx_n = sb("ctx_n", [P, 2, P])
        att_y = sb("att_y", [P, 2, P])
        tail_bn = sb("tail_bn", [P, 2, 6])
        tail_mv = sb("tail_mv", [P, 2, 2])
        tail_xc = sb("tail_xc", [P, 2, P])
        tail_ve = sb("tail_ve", [P, 2])
        tail_rs = sb("tail_rs", [P, 2])
        tail_n = sb("tail_n", [P, 2, P])
        tail_g = sb("tail_g", [P, 2, P])
        xn_bv = [sb(f"xn_bv{i}", [P, TT, P]) for i in range(2)]
        x1_beta = [sb(f"x1_beta{i}", [P, TT, P]) for i in range(2)]

        ps_z = [bank(f"ps_z{i}") for i in range(2)]
        ps_s = [bank(f"ps_s{i}") for i in range(2)]
        ps_t = [bank(f"ps_t{i}") for i in range(2)]
        ps_c = bank("ps_c")
        ps_m = bank("ps_m")

        s_ffn_in = sem("ffn_params_loaded")
        s_proj_in = sem("projections_loaded")
        s_norm_in = sem("gamma_beta_bv_loaded")
        s_tile1 = sem("tile1_loaded")
        s_x0 = sem("x0_loaded")
        s_out = sem("out_stored")
        s_const = sem("consts_made")
        s_setd = sem("setup_vector")
        s_setp = sem("setup_pool")
        s_wt = sem("wt_transposed")
        s_wthi = sem("wt_hi_made")
        s_w1 = sem("w1_made")
        f_bn, f_mv, f_rs, f_xn = sem("ffn_bn_done"), sem("ffn_mv_done"), sem("ffn_rstd_steps"), sem("ffn_xn_done")
        z_full, z_hi, z_free = sem("z_full"), sem("z_hi_made"), sem("z_free")
        a_bn, a_mv, a_rs, a_xn = sem("att_bn_done"), sem("att_mv_done"), sem("att_rstd_steps"), sem("att_xn_done")
        m_full, m_hi, m_free = sem("misc_full"), sem("misc_hi_made"), sem("misc_free")
        mt_full, mt_free = sem("max_transposed"), sem("max_copied")
        s_spread = sem("rows_spread")
        s_full, s_max = sem("scores_full"), sem("max_done")
        s_mparts = sem("max_parts_made")
        s_mrows = sem("max_rows_placed")
        t_full, s_exp = sem("shifted_scores_full"), sem("exp_done")
        c_full, c_free = sem("context_full"), sem("context_copied")
        s_den = sem("den_inverted")
        s_y = sem("att_y_done")
        t_bn, t_mv, t_rs = sem("tail_bn_done"), sem("tail_mv_done"), sem("tail_rstd_steps")
        t_n = sem("tail_steps")
        s_x2 = sem("x2_done")
        s_base = sem("tail_base_done")

        def full(t, r):
            return Iteration(t, r, ffn_a=2 * t, ffn_b=2 * t + 1, next_a=2 * t + 2, misc_base=8 * t)

        head = [Iteration(0, 0, prev=False, ffn_b=2, misc_base=4, load=False),
                Iteration(1, 1, ffn_b=3, next_a=4, misc_base=8)]
        LOOP_FROM, LOOP_TO = 2, TILES - 2
        T = TILES
        tail = [Iteration(T - 2, 0, ffn_a=2 * (T - 2), next_a=2 * (T - 2) + 1, misc_base=8 * (T - 2)),
                Iteration(T - 1, 1, prep=False, ffn_a=2 * (T - 2) + 1, next_a=2 * (T - 2) + 2,
                          misc_base=8 * (T - 1)),
                Iteration(T, 0, cur=False, prep=False, ffn_a=2 * (T - 2) + 2,
                          next_a=2 * (T - 2) + 3, misc_base=8 * (T - 1) + 4)]
        LAST_FFN = 2 * T - 1
        assert (LOOP_TO - LOOP_FROM) % 2 == 0 and LOOP_FROM % 2 == 0

        def run(eng, steps):
            for it in head:
                steps(it)
            with eng.Fori(0, (LOOP_TO - LOOP_FROM) // 2) as pair:
                for r in range(2):
                    steps(full(pair * 2 + (LOOP_FROM + r), r))
            for it in tail:
                steps(it)

        CONST_IDENT, CONST_NORM, CONSTS = 4, 8, 14
        SETD_W0, SETD_FFN, SETD_SQUARES, SETD_BOUND, SETD_FIT, SETD_ALL = 7, 11, 13, 15, 19, 24
        AT_WT, AT_WT_HI, AT_WT_LO = 11, 12, 13
        FIRST = {7: "LNT", 8: "Q", 9: "K", 10: "V"}

        def first_ffn(tile):
            return tile if isinstance(tile, int) and tile <= 3 else 2 * tile - 3

        def unit(u):
            return u // HALF, u // LANES % GROUPS, u % LANES

        def at_least(eng, s, n):
            if not isinstance(n, int) or n > 0:
                eng.wait_ge(s, n)

        block = ctx.enter_context(nc.Block())

        @block.sync
        def _(sp):
            def start_of(t):
                return t * (TILE * P) if isinstance(t, int) else sp.snap(t * (TILE * P))

            def tile_rows(flat, start):
                return flat[bass.ds(start, TILE * P)].rearrange("(b p a d) -> p b a d", b=2, p=P, a=2)

            def load_x(start):
                sp.dma_start(x0[:].rearrange("p (b a) d -> p b a d", b=2), tile_rows(x_flat, start)).then_inc(s_x0, 16)

            def store_x3(start):
                sp.dma_start(tile_rows(out_flat, start), x3[:].rearrange("p (b a) d -> p b a d", b=2)).then_inc(s_out, 16)

            def spread(par, lo, hi):
                n = 0
                for w, rows in ((0, q_rows), (1, k_rows)):
                    for part in range(PARTS):
                        src = (qk_lo if part == (2, 1)[w] else qk_hi)[w]
                        for j in range(LANES):
                            if lo <= n < hi:
                                sp.dma_start(rows[par][ROWS * j + HD * part:ROWS * j + HD * (part + 1), :, :],
                                             src[ROWS * j:ROWS * (j + 1), :]).then_inc(s_spread, 16)
                            n += 1

            def place_max(t, par, hb):
                sp.wait_ge(mt_free, 4 * t + hb + 1)
                b, g0 = hb // 2, 2 * (hb % 2)
                for j in range(LANES):
                    r = ROWS * j + HD * PARTS
                    sp.dma_start(q_rows[par][r:r + 2, g0:g0 + 2, b * SEQ:(b + 1) * SEQ],
                                 max_rows[4 * j:4 * j + 4, :]).then_inc(s_mrows, 16)

            load_x(start_of(0))
            for i, scale in enumerate((s0, s1, s2)):
                sp.dma_start(s_raw[:, i:i + 1], scale.partition_broadcast(P)).then_inc(s_ffn_in, 16)
            for dst, src in ((k0_raw, k0), (k1_raw, k1), (k2_raw, k2)):
                sp.dma_start(dst[:], src.rearrange("(c p) n -> p c n", p=P)).then_inc(s_ffn_in, 16)
            for i, w in enumerate((wq, wk, wv)):
                sp.dma_start(w_raw[:, i, :], w).then_inc(s_proj_in, 16)
            for i, b in enumerate((bq, bk, bv)):
                sp.dma_start(b_raw[:, i:i + 1], b.rearrange("(n a) -> n a", a=1)).then_inc(s_proj_in, 16)
            sp.dma_start(x3[:].rearrange("p (b a) d -> p b a d", b=2), tile_rows(x_flat, start_of(1))).then_inc(s_tile1, 16)
            for dst, src in ((gamma_b, gamma), (beta_b, beta), (bv_b, bv)):
                sp.dma_start(dst[:], src.partition_broadcast(P)).then_inc(s_norm_in, 16)
            sp.wait_ge(z_free, Z_USES)
            load_x(start_of(2))
            sp.wait_ge(m_free, 3)
            sp.wait_ge(s_const, CONSTS)
            spread(0, 0, SPREADS)

            def steps(it):
                t, par = it.t, it.par
                if it.ffn_b is not None and it.load:
                    start = start_of(t + 2)
                    sp.wait_ge(z_free, Z_USES * (first_ffn(t + 1) + 1))
                    load_x(start)
                if it.prev:
                    place_max(t - 1, 1 - par, 3)
                if it.cur:
                    place_max(t, par, 0)
                if it.ffn_a is not None:
                    start = start_of(t - 2)
                    sp.wait_ge(z_free, Z_USES * it.ffn_a + Z_USES)
                    store_x3(start)
                if it.prep:
                    sp.wait_ge(m_free, it.misc["K"] + 1)
                    if it.prev:
                        sp.wait_ge(t_full, UNITS * t + 1)
                    spread(1 - par, 0, 6)
                if it.cur:
                    place_max(t, par, 1)
                if it.prep:
                    spread(1 - par, 6, SPREADS)
                if it.cur:
                    place_max(t, par, 2)

            run(sp, steps)
            sp.wait_ge(z_free, Z_USES * (LAST_FFN + 1))
            store_x3(start_of(TILES - 1))
            sp.wait_ge(s_out, 16 * TILES)

        @block.gpsimd
        def _(pool):
            g = nc.gpsimd
            g.memset(ident[:], 0.0).then_inc(s_const, 1)
            g.memset(ident16[:], 0.0).then_inc(s_const, 1)
            pool.wait_ge(s_const, 2)
            for m in (ident, ident16):
                g.affine_select(out=m[:], in_=m[:], compare_op=ALU.not_equal, fill=1.0, base=0,
                                pattern=[[-1, P]], channel_multiplier=1).then_inc(s_const, 1)
            g.memset(minus_half[:], -0.5).then_inc(s_const, 1)
            g.memset(plus_half[:], 0.5).then_inc(s_const, 1)
            g.memset(eps[:], EPS).then_inc(s_const, 1)
            pool.wait_ge(s_const, CONST_IDENT)
            for j in range(LANES):
                last = g.tensor_copy(lane_order[:].rearrange("p (j i g) -> p j i g", j=LANES, g=GROUPS)[:, j],
                                     ident[:].rearrange("p (g j i) -> p j i g", j=LANES, g=GROUPS)[:, j])
            last.then_inc(s_const, 1)

            def normalize(dst, src, mv, xc, ve, rs, n, steps_done, k, done):
                shape = [P, n, P]
                g.tensor_tensor(ve[:], mv[:, :, 1], eps[:, 0:n], ALU.add).then_inc(steps_done, 1)
                g.tensor_tensor(xc[:], src, mv[:, :, 0:1].broadcast_to(shape), ALU.subtract)
                pool.wait_ge(steps_done, k + 1)
                g.tensor_tensor(rs[:], ve[:], minus_half[:, 0:n], ALU.pow).then_inc(steps_done, 1)
                pool.wait_ge(steps_done, k + 2)
                g.tensor_tensor(dst, xc[:], rs[:].unsqueeze(2).broadcast_to(shape), ALU.mult).then_inc(done, 1)

            def ffn_norm(f, src):
                at_least(pool, z_full, Z_USES * f - (Z_USES - 1))
                pool.wait_ge(f_mv, f + 1)
                normalize(ffn_xn[:], src[:], ffn_mv, ffn_xc, ffn_ve, ffn_rs, TT, f_rs, 2 * f, f_xn)

            def att_norm(t, par):
                pool.wait_ge(a_mv, t + 1)
                normalize(att_xn[par][:], x1[par][:], att_mv, att_xc, att_ve, att_rs, TT, a_rs, 2 * t, a_xn)

            def tail_y(t, b, par, use):
                pool.wait_ge(s_base, t + 1)
                pool.wait_ge(m_free, use + 1)
                g.tensor_tensor(att_y[:], ctx_n[:], xn_bv[par][:, 2 * b:2 * b + 2, :], ALU.add).then_inc(s_y, 1)

            def tail_norm(t, b, par):
                n = 2 * t + b
                pool.wait_ge(t_mv, n + 1)
                normalize(tail_n[:], att_y[:], tail_mv, tail_xc, tail_ve, tail_rs, 2, t_rs, 2 * n, t_n)
                pool.wait_ge(t_n, 2 * n + 1)
                g.tensor_tensor(tail_g[:], tail_n[:], gamma_b[:].unsqueeze(1).broadcast_to([P, 2, P]),
                                ALU.mult).then_inc(t_n, 1)
                pool.wait_ge(t_n, 2 * n + 2)
                g.tensor_tensor(x2[par][:, 2 * b:2 * b + 2, :], tail_g[:], x1_beta[par][:, 2 * b:2 * b + 2, :],
                                ALU.add).then_inc(s_x2, 1)

            def tail_base(t, par):
                at_least(pool, s_x2, 2 * (t - 1))
                g.tensor_tensor(x1_beta[par][:], x1[par][:], beta_b[:].unsqueeze(1).broadcast_to([P, TT, P]), ALU.add)
                g.tensor_tensor(xn_bv[par][:], att_xn[par][:], bv_b[:].unsqueeze(1).broadcast_to([P, TT, P]),
                                ALU.add).then_inc(s_base, 1)

            pool.wait_ge(s_const, CONST_NORM)
            ffn_norm(0, x0)
            pool.wait_ge(s_setd, SETD_SQUARES)
            g.tensor_tensor(w_norm[:], w_bound[:], plus_half[:], ALU.pow).then_inc(s_setp, 1)
            pool.wait_ge(s_setd, SETD_BOUND)
            g.partition_all_reduce(w_most[:], w_inv[:], P, RMAX).then_inc(s_setp, 1)
            ffn_norm(1, x3)
            for i in range(2):
                g.memset(k_rows[i][:], -1.0 / M_UNIT).then_inc(s_const, 1)
                g.memset(v_cols[i][:], 0.0).then_inc(s_const, 1)
            pool.wait_ge(s_const, CONSTS - 2)
            for i in range(2):
                g.memset(v_cols[i][:, :, :, HD:HD + 1], 1.0).then_inc(s_const, 1)
            att_norm(0, 0)
            pool.wait_ge(s_norm_in, 16 * 3)

            def steps(it):
                t, par = it.t, it.par
                if it.prep:
                    att_norm(t + 1, 1 - par)
                if it.ffn_b is not None:
                    ffn_norm(it.ffn_b, x0)
                if it.prev:
                    tail_y(t - 1, 0, 1 - par, it.misc["CT01"])
                    tail_norm(t - 1, 0, 1 - par)
                if it.cur:
                    tail_base(t, par)
                if it.prev:
                    tail_y(t - 1, 1, 1 - par, it.misc["CT11"])
                    tail_norm(t - 1, 1, 1 - par)
                if it.next_a is not None:
                    ffn_norm(it.next_a, x2[1 - par])

            run(pool, steps)

        @block.tensor
        def _(pe):
            def bank_of(use):
                return ps_z[use % 2]

            def ffn_transpose(f):
                at_least(pe, z_free, Z_USES * f - 1)
                pe.wait_ge(f_xn, f + 1)
                for i in range(TT):
                    last = pe.transpose(bank_of(0)[:, i * P:(i + 1) * P], ffn_xn[:, i, :], ident[:])
                last.then_inc(z_full, 1)

            def ffn_in(f, m):
                pe.wait_ge(z_free, Z_USES * f + 1 + max(0, m - 1))
                o = bank_of(1 + m)
                pe.matmul(o[:], w0[:, m * P:(m + 1) * P], ffn_hi[:, 0, :], start=True, stop=False)
                pe.matmul(o[:], w0[:, m * P:(m + 1) * P], ffn_lo[:, 0, :], start=False, stop=True).then_inc(z_full, 1)

            def ffn_mid(f, n):
                m, k = n // KC, n % KC
                o = bank_of(5 + m)
                pe.wait_ge(z_free, Z_USES * f + max(2 + k, 4 + m))
                w = w1[:, k, m * P:(m + 1) * P]
                pe.matmul(o[:], w, ffn_hi[:, 1 + k, :], start=(k == 0), stop=False)
                last = pe.matmul(o[:], w, ffn_lo[:, 1 + k, :], start=False, stop=(k == KC - 1))
                if k == KC - 1:
                    last.then_inc(z_full, 1)

            def ffn_out(f, i, k):
                o = bank_of(9)[:, i * P:(i + 1) * P]
                if i == 0:
                    pe.wait_ge(z_free, Z_USES * f + max(6 + k, 8))
                pe.matmul(o, ffn_hi[:, 5 + k, i * P:(i + 1) * P], w2[:, k, :], start=(i == 0 and k == 0),
                          stop=False)
                last = pe.matmul(o, ffn_lo[:, 5 + k, i * P:(i + 1) * P], w2[:, k, :], start=False,
                                 stop=(i == TT - 1 and k == KC - 1))
                if i == TT - 1 and k == KC - 1:
                    last.then_inc(z_full, 1)

            def ffn_piece(f, s):
                if s == 0:
                    ffn_transpose(f)
                elif s in FFN_IN:
                    ffn_in(f, FFN_IN[s])
                for at, lo, hi in FFN_MID:
                    if s == at:
                        for n in range(lo, hi):
                            ffn_mid(f, n)
                if s in (12, 13):
                    for i in (2 * (s - 12), 2 * (s - 12) + 1):
                        for k in range(KC - 1):
                            ffn_out(f, i, k)
                elif s == 14:
                    for i in range(TT):
                        ffn_out(f, i, KC - 1)

            def misc_wait(use):
                at_least(pe, m_free, use)

            def att_transpose(t, par, use):
                misc_wait(use)
                pe.wait_ge(a_xn, t + 1)
                for i in range(TT):
                    last = pe.transpose(ps_m[:, i * P:(i + 1) * P], att_xn[par][:, i, :], ident[:])
                last.then_inc(m_full, 1)

            def project(w, use):
                misc_wait(use)
                n = 0
                for ww in (wt_hi, wt_lo):
                    for xx in (att_hi, att_lo):
                        last = pe.matmul(ps_m[:], ww[:, w, :], xx[:], start=(n == 0), stop=(n == 3))
                        n += 1
                last.then_inc(m_full, 1)

            def project_v(use):
                misc_wait(use)
                for i in range(TT):
                    n = 0
                    for xx in (att_hi, att_lo):
                        for ww in (wt_hi, wt_lo):
                            last = pe.matmul(ps_m[:, i * P:(i + 1) * P], xx[:, i * P:(i + 1) * P], ww[:, 2, :],
                                             start=(n == 0), stop=(n == 3))
                            n += 1
                last.then_inc(m_full, 1)

            def scores(t, par, u):
                b, g, j = unit(u)
                n = UNITS * t + u
                if u == 0:
                    pe.wait_ge(s_spread, 16 * SPREADS * (t + 1))
                at_least(pe, s_max, n - 1)
                r = slice(ROWS * j, ROWS * j + HD * PARTS)
                for a in range(2):
                    c = b * SEQ + a * P
                    last = pe.matmul(ps_s[u % 2][:, a * SEQ:(a + 1) * SEQ], q_rows[par][r, g, c:c + P],
                                     k_rows[par][r, g, b * SEQ:(b + 1) * SEQ], start=True, stop=True)
                last.then_inc(s_full, 1)

            def shifted(t, par, u):
                b, g, j = unit(u)
                n = UNITS * t + u
                if u % HB == 0:
                    pe.wait_ge(s_mrows, 64 * (4 * t + u // HB + 1))
                at_least(pe, s_exp, n - 1)
                r = slice(ROWS * j, ROWS * j + HD * PARTS + 2)
                for a in range(2):
                    c = b * SEQ + a * P
                    last = pe.matmul(ps_t[u % 2][:, a * SEQ:(a + 1) * SEQ], k_rows[par][r, g, c:c + P],
                                     q_rows[par][r, g, b * SEQ:(b + 1) * SEQ], start=True, stop=True)
                last.then_inc(t_full, 1)

            def context(t, par, grp):
                b, g = grp // GROUPS, grp % GROUPS
                n = 2 * GROUPS * t + grp
                pe.wait_ge(s_exp, LANES * n + LANES)
                at_least(pe, c_free, n)
                last_tile = isinstance(t, int) and t == TILES - 1
                pe.wait_ge(mt_free, 4 * t + (min(4, 2 + grp // 2) if last_tile else 2 + grp // 2))
                for a in range(2):
                    for j in range(LANES):
                        last = pe.matmul(ps_c[ROWS * j:ROWS * (j + 1), 0:SEQ], v_cols[par][:, 2 * b + a, LANES * g + j, :],
                                         probs[grp % 2][:, j, a * SEQ:(a + 1) * SEQ], start=(a == 0), stop=(a == 1))
                last.then_inc(c_full, 1)

            def context_transpose(t, b, a, use):
                misc_wait(use)
                pe.wait_ge(c_free, 2 * GROUPS * t + GROUPS * (b + 1))
                for g in range(GROUPS):
                    last = pe.transpose(ps_m[:, g * P:(g + 1) * P], ctx_t[:, GROUPS * b + g, a * P:(a + 1) * P], ident[:])
                last.then_inc(m_full, 1)

            def max_transpose(t, hb):
                at_least(pe, c_free, 2 * GROUPS * t + 2 * hb - 2)
                at_least(pe, mt_free, 4 * t + hb)
                pe.wait_ge(s_mparts, 2 * (4 * t + hb + 1))
                for a in range(2):
                    last = pe.transpose(ps_c[:].bitcast(F16)[0:4 * LANES, 2 * SEQ + a * P:2 * SEQ + (a + 1) * P],
                                        max_parts[:, a * LANES:(a + 1) * LANES].rearrange("p j c g -> p (j c g)"),
                                        ident16[:])
                last.then_inc(mt_full, 1)

            def project_weights():
                pe.wait_ge(s_setd, SETD_FIT)
                for i, order in enumerate((lane_order, lane_order, ident)):
                    pe.matmul(ps_c[:, i * P:(i + 1) * P], w_fit[:, i, :], order[:], start=True, stop=True)
                for i in range(2):
                    last = pe.matmul(ps_c[:, 3 * P + i:3 * P + i + 1], lane_order[:], b_raw[:, i:i + 1],
                                     start=True, stop=True)
                last.then_inc(s_wt, 1)

            pe.wait_ge(s_const, CONST_NORM)
            for s in range(16):
                if s == 1:
                    pe.wait_ge(s_setd, SETD_FFN)
                    pe.wait_ge(s_w1, 1)
                ffn_piece(0, s)
                if s == AT_WT:
                    project_weights()
            pe.wait_ge(s_setd, SETD_ALL)
            for s in range(16):
                ffn_piece(1, s)
                what = FIRST.get(s)
                if what == "LNT":
                    att_transpose(0, 0, 0)
                elif what == "Q":
                    project(0, 1)
                elif what == "K":
                    project(1, 2)
                elif what == "V":
                    project_v(3)

            def steps(it):
                t, par = it.t, it.par
                for s in range(UNITS):
                    if it.cur:
                        scores(t, par, s)
                    if s < HALF:
                        if it.prev:
                            shifted(t - 1, 1 - par, s + HALF)
                    elif it.cur:
                        shifted(t, par, s - HALF)
                    if it.prev and s in (1, 5, 9, 13, 17):
                        context(t - 1, 1 - par, s // 4 + 3)
                    if it.cur and s in (21, 25, 29):
                        context(t, par, (s - 21) // 4)
                    if s < HALF and it.ffn_a is not None:
                        ffn_piece(it.ffn_a, s)
                    if s >= HALF and it.ffn_b is not None:
                        ffn_piece(it.ffn_b, s - HALF)
                    if it.prev:
                        if s == AT_MAX[3]:
                            max_transpose(t - 1, 3)
                        for b, a in ((0, 0), (0, 1), (1, 0), (1, 1)):
                            if s == AT[f"CT{b}{a}"]:
                                context_transpose(t - 1, b, a, it.misc[f"CT{b}{a}"])
                    if it.cur:
                        for hb in range(3):
                            if s == AT_MAX[hb]:
                                max_transpose(t, hb)
                    if it.prep:
                        if s == AT["LNT"]:
                            att_transpose(t + 1, 1 - par, it.misc["LNT"])
                        if s == AT["Q"]:
                            project(0, it.misc["Q"])
                        if s == AT["K"]:
                            project(1, it.misc["K"])
                        if s == AT["V"]:
                            project_v(it.misc["V"])

            run(pe, steps)
            for s in range(16):
                ffn_piece(LAST_FFN, s)

        @block.scalar
        def _(act):
            a_ = nc.scalar

            def z_split(f, use):
                act.wait_ge(z_full, Z_USES * f + use + 1)
                a_.activation(ffn_hi[:, use, :], ps_z[use % 2][:], ACT.Relu if use else ACT.Copy,
                              scale=1.0 if use else XN_SCALE).then_inc(z_hi, 1)

            def ffn_piece(f, s):
                if s == 0:
                    z_split(f, 0)
                elif s in FFN_IN:
                    z_split(f, 1 + FFN_IN[s])
                elif s in FFN_MID_DONE:
                    z_split(f, 5 + FFN_MID_DONE[s])

            def att_split(use):
                act.wait_ge(m_full, use + 1)
                a_.activation(att_hi[:], ps_m[:], ACT.Copy, scale=XN_SCALE).then_inc(m_hi, 1)

            def qk_split(w, use):
                act.wait_ge(m_full, use + 1)
                a_.activation(qk_hi[w][:], ps_m[:], ACT.Identity, bias=b_fit[:, w:w + 1]).then_inc(m_hi, 1)

            def v_copy(t, par, use):
                act.wait_ge(m_full, use + 1)
                at_least(act, c_full, 2 * GROUPS * (t - 1))
                a_.activation(v_cols[par][:].rearrange("p t h r -> p (t h) r")[:, :, 0:HD],
                              ps_m[:].rearrange("p (n i) -> p n i", i=HD), ACT.Copy,
                              scale=v_unscale[:, 0:1]).then_inc(m_free, 1)

            def exps(t, u):
                n = UNITS * t + u
                grp = u // LANES
                act.wait_ge(t_full, n + 1)
                if u % LANES == 0:
                    at_least(act, c_full, 2 * GROUPS * t + grp - 1)
                a_.activation(probs[grp % 2][:, u % LANES, :], ps_t[u % 2][:], ACT.Exp,
                              scale=score_scale[:, 0:1]).then_inc(s_exp, 1)

            def context_copy(t, grp):
                act.wait_ge(c_full, 2 * GROUPS * t + grp + 1)
                a_.activation(ctx_t[:, grp, :], ps_c[:, 0:SEQ], ACT.Copy).then_inc(c_free, 1)

            act.wait_ge(s_setd, SETD_W0)
            a_.activation(w1[:], k1_raw[:], ACT.Identity, bias=w1_scale[:, 1:2], scale=w1_scale[:, 0:1]).then_inc(s_w1, 1)
            for s in range(16):
                ffn_piece(0, s)
                if s == AT_WT_HI:
                    act.wait_ge(s_wt, 1)
                    a_.activation(wt_hi[:].rearrange("p i n -> p (i n)"), ps_c[:, 0:3 * P], ACT.Copy).then_inc(s_wthi, 1)
            act.wait_ge(s_setd, SETD_ALL)
            for s in range(16):
                ffn_piece(1, s)
                what = FIRST.get(s)
                if what == "LNT":
                    att_split(0)
                elif what == "Q":
                    qk_split(0, 1)
                elif what == "K":
                    qk_split(1, 2)
                elif what == "V":
                    act.wait_ge(s_const, CONSTS)
                    v_copy(0, 0, 3)

            def steps(it):
                t, par = it.t, it.par
                for s in range(UNITS):
                    if s < HALF:
                        if it.prev:
                            exps(t - 1, s + HALF)
                    elif it.cur:
                        exps(t, s - HALF)
                    if s < HALF and it.ffn_a is not None:
                        ffn_piece(it.ffn_a, s)
                    if s >= HALF and it.ffn_b is not None:
                        ffn_piece(it.ffn_b, s - HALF)
                    if it.prev and s in (1, 5, 9, 13, 17):
                        context_copy(t - 1, s // 4 + 3)
                    if it.cur and s in (21, 25, 29):
                        context_copy(t, (s - 21) // 4)
                    if it.prep:
                        if s == AT["LNT"]:
                            att_split(it.misc["LNT"])
                        if s == AT["Q"]:
                            qk_split(0, it.misc["Q"])
                        if s == AT["K"]:
                            qk_split(1, it.misc["K"])
                        if s == AT["V"]:
                            v_copy(t + 1, 1 - par, it.misc["V"])

            run(act, steps)
            for s in range(16):
                ffn_piece(LAST_FFN, s)

        @block.vector
        def _(dve):
            v = nc.vector
            done = [0]

            def step(ins):
                done[0] += 1
                ins.then_inc(s_setd, 1)

            def so_far():
                dve.wait_ge(s_setd, done[0])

            def setup_ffn():
                dve.wait_ge(s_ffn_in, 16 * 6)
                step(v.tensor_scalar(s_tmp[:, 0:2], s_raw[:, 0:2], 0.0, None, ALU.is_ge))
                so_far()
                step(v.tensor_scalar(s_sign[:], s_tmp[:, 0:2], 2.0, -1.0, ALU.mult, ALU.add))
                so_far()
                step(v.tensor_scalar(w0_scale[:], s_sign[:, 0:1], W0_UNIT, None, ALU.mult))
                step(v.tensor_scalar(w1_scale[:, 0:1], s_sign[:, 1:2], 2 * W1_UNIT, None, ALU.mult))
                step(v.tensor_scalar(w1_scale[:, 1:2], s_sign[:, 1:2], -W1_UNIT, None, ALU.mult))
                step(v.tensor_tensor(s_tmp[:, 2:4], s_raw[:, 0:2], s_sign[:], ALU.mult))
                step(v.tensor_tensor(w0_diff[:], k0_raw[:, 0, :], k0_raw[:, 1, :], ALU.subtract))
                so_far()
                assert done[0] == SETD_W0
                step(v.tensor_scalar(w0[:], w0_diff[:], w0_scale[:, 0:1], None, ALU.mult))
                step(v.tensor_scalar(score_tmp[:], s_tmp[:, 2:3], s_tmp[:, 3:4], FFN_OUT, ALU.mult, ALU.mult))
                step(v.tensor_scalar(w2[:], k2_raw[:], 2.0, -1.0, ALU.mult, ALU.add))
                so_far()
                step(v.tensor_tensor(ffn_scale[:], score_tmp[:], s_raw[:, 2:3], ALU.mult))
                assert done[0] == SETD_FFN

            def setup_squares():
                dve.wait_ge(s_proj_in, 16 * 6)
                step(v.tensor_tensor(w_sq[:], w_raw[:], w_raw[:], ALU.mult))
                so_far()
                step(v.tensor_reduce(w_bound[:], w_sq[:], AX.X, ALU.add))
                assert done[0] == SETD_SQUARES

            def setup_bound():
                step(v.scalar_tensor_tensor(out=b_abs[:], in0=b_raw[:], scalar=-1.0, in1=b_raw[:], op0=ALU.mult, op1=ALU.max))
                so_far()
                dve.wait_ge(s_setp, 1)
                step(v.scalar_tensor_tensor(out=w_inv[:], in0=w_norm[:], scalar=float(P) ** 0.5, in1=b_abs[:],
                                            op0=ALU.mult, op1=ALU.add))
                assert done[0] == SETD_BOUND

            def setup_fit():
                dve.wait_ge(s_setp, 2)
                step(v.tensor_scalar(w_norm[:], w_most[:], 1e-30, None, ALU.max))
                so_far()
                step(v.reciprocal(w_inv[:], w_norm[:]))
                so_far()
                step(v.tensor_scalar(w_factor[:], w_inv[:], Q_MAX, None, ALU.mult))
                so_far()
                for i in range(3):
                    last = v.tensor_scalar(w_fit[:, i, :], w_raw[:, i, :], w_factor[:, i:i + 1], 1.0 / XN_SCALE,
                                           ALU.mult, ALU.mult)
                step(last)
                assert done[0] == SETD_FIT

            def setup_projections():
                step(v.tensor_scalar(score_tmp[:], w_norm[:, 0:1], w_norm[:, 1:2], Q_MAX ** -2, ALU.mult, ALU.mult))
                so_far()
                step(v.tensor_scalar(score_scale[:], score_tmp[:], float(1.0 / np.sqrt(HD)), None, ALU.mult))
                step(v.tensor_scalar(v_unscale[:], w_norm[:, 2:3], 1.0 / Q_MAX, None, ALU.mult))
                dve.wait_ge(s_wthi, 1)
                step(v.tensor_tensor(b_fit[:, 0:2], ps_c[:, 3 * P:3 * P + 2], w_factor[:, 0:2], ALU.mult))
                step(v.tensor_tensor(wt_lo[:].rearrange("p i n -> p (i n)"), ps_c[:, 0:3 * P],
                                     wt_hi[:].rearrange("p i n -> p (i n)"), ALU.subtract))
                assert done[0] == SETD_ALL
                so_far()

            def stats(src, bn, n, bn_done):
                for i in range(n):
                    last = v.bn_stats(bn[:, i, :], src[:, i, :])
                last.then_inc(bn_done, 1)

            def mean_var(bn, mv, n, mv_done):
                for i in range(n):
                    last = v.bn_aggr(mv[:, i, :], bn[:, i, :])
                last.then_inc(mv_done, 1)

            def ffn_stats(src):
                stats(src, ffn_bn, TT, f_bn)

            def ffn_mean_var(f):
                mean_var(ffn_bn, ffn_mv, TT, f_mv)

            def ffn_mean_var_wait(f):
                at_least(dve, f_xn, f)
                dve.wait_ge(f_bn, f + 1)

            def z_rest(f, use):
                dve.wait_ge(z_hi, 9 * f + use + 1)
                if use:
                    v.scalar_tensor_tensor(out=ffn_lo[:, use, :], in0=ps_z[use % 2][:], scalar=0.0,
                                           in1=ffn_hi[:, use, :], op0=ALU.max, op1=ALU.subtract).then_inc(z_free, 1)
                else:
                    v.scalar_tensor_tensor(out=ffn_lo[:, 0, :], in0=ps_z[0][:], scalar=XN_SCALE,
                                           in1=ffn_hi[:, 0, :], op0=ALU.mult, op1=ALU.subtract).then_inc(z_free, 1)

            def ffn_residual(f, src, dst, stored=None, based=None):
                dve.wait_ge(z_full, Z_USES * f + Z_USES)
                if based is not None:
                    dve.wait_ge(s_base, based)
                if stored is not None:
                    at_least(dve, s_out, 16 * stored)
                v.scalar_tensor_tensor(out=dst[:].rearrange("p t d -> p (t d)"), in0=ps_z[1][:],
                                       scalar=ffn_scale[:, 0:1], in1=src[:].rearrange("p t d -> p (t d)"),
                                       op0=ALU.mult, op1=ALU.add).then_inc(z_free, 1)

            def ffn_piece(f, s, src, dst, stored=None, based=None):
                if s == 0:
                    z_rest(f, 0)
                elif s in FFN_IN:
                    z_rest(f, 1 + FFN_IN[s])
                elif s in FFN_MID_DONE:
                    z_rest(f, 5 + FFN_MID_DONE[s])
                elif s == FFN_RESIDUAL:
                    ffn_residual(f, src, dst, stored, based)

            def att_stats(par, f):
                dve.wait_ge(z_free, Z_USES * (f + 1))
                stats(x1[par], att_bn, TT, a_bn)

            def att_mean_var_wait(t):
                at_least(dve, a_xn, t)
                dve.wait_ge(a_bn, t + 1)

            def att_rest(t):
                dve.wait_ge(m_hi, 3 * t + 1)
                v.scalar_tensor_tensor(out=att_lo[:], in0=ps_m[:], scalar=XN_SCALE, in1=att_hi[:],
                                       op0=ALU.mult, op1=ALU.subtract).then_inc(m_free, 1)

            def qk_rest(t, w):
                dve.wait_ge(m_hi, 3 * t + 2 + w)
                v.scalar_tensor_tensor(out=qk_lo[w][:], in0=ps_m[:], scalar=b_fit[:, w:w + 1], in1=qk_hi[w][:],
                                       op0=ALU.add, op1=ALU.subtract).then_inc(m_free, 1)

            def row_maxima(t, u):
                b, g, j = unit(u)
                dve.wait_ge(s_full, UNITS * t + u + 1)
                if u % HB == 0:
                    at_least(dve, s_mparts, 2 * (4 * t + u // HB))
                v.tensor_reduce(row_max[:, j::LANES, g % 2],
                                ps_s[u % 2][:].rearrange("p (a k) -> p a k", a=2), AX.X, ALU.max).then_inc(s_max, 1)

            def split_max(t, hb):
                n = 4 * t + hb
                dve.wait_ge(s_max, UNITS * t + HB * (hb + 1))
                v.tensor_scalar(max_parts[:, :, 0, :], row_max[:], M_UNIT, None, ALU.mult).then_inc(s_mparts, 1)
                dve.wait_ge(s_mparts, 2 * n + 1)
                v.scalar_tensor_tensor(out=max_parts[:, :, 1, :], in0=row_max[:], scalar=M_UNIT,
                                       in1=max_parts[:, :, 0, :], op0=ALU.mult, op1=ALU.subtract).then_inc(s_mparts, 1)

            def copy_max(t, hb):
                dve.wait_ge(mt_full, 4 * t + hb + 1)
                at_least(dve, s_mrows, 64 * (4 * t + hb))
                v.tensor_copy(max_rows[:], ps_c[:].bitcast(F16)[0:4 * LANES, 2 * SEQ:3 * SEQ]).then_inc(mt_free, 1)

            def context_norm(t, b, a, use):
                n = 4 * t + 2 * b + a
                dve.wait_ge(m_full, use + 1)
                c = ps_m[:].rearrange("p (h r) -> p h r", r=ROWS)
                v.reciprocal(den[:], c[:, :, HD]).then_inc(s_den, 1)
                dve.wait_ge(s_den, n + 1)
                at_least(dve, s_y, 2 * t + b)
                v.tensor_tensor(ctx_n[:, a, :].rearrange("p (h i) -> p h i", i=HD), c[:, :, 0:HD],
                                den[:].unsqueeze(2).broadcast_to([P, HEADS, HD]), ALU.mult).then_inc(m_free, 1)

            def tail_stats(t, b):
                dve.wait_ge(s_y, 2 * t + b + 1)
                stats(att_y, tail_bn, 2, t_bn)

            dve.wait_ge(s_x0, 16)
            ffn_stats(x0)
            ffn_mean_var_wait(0)
            ffn_mean_var(0)
            setup_ffn()
            for s in range(16):
                ffn_piece(0, s, x0, x1[0])
                if s == 0:
                    setup_squares()
                elif s == 2:
                    setup_bound()
                elif s == 5:
                    setup_fit()
                elif s == 8:
                    dve.wait_ge(s_tile1, 16)
                    ffn_stats(x3)
                elif s == 10:
                    ffn_mean_var_wait(1)
                    ffn_mean_var(1)
                elif s == AT_WT_LO:
                    setup_projections()
            att_stats(0, 0)
            att_mean_var_wait(0)
            mean_var(att_bn, att_mv, TT, a_mv)
            for s in range(16):
                ffn_piece(1, s, x3, x1[1])
                what = FIRST.get(s)
                if what == "LNT":
                    att_rest(0)
                elif what == "Q":
                    qk_rest(0, 0)
                elif what == "K":
                    qk_rest(0, 1)

            def steps(it):
                t, par = it.t, it.par
                for s in range(UNITS):
                    norm_prep = it.prep and s == AT_STATS_PREP + 1
                    norm_b = it.ffn_b is not None and s == AT_STATS_B + 1
                    norm_a = it.next_a is not None and s == AT_STATS_A + 1
                    norm_tail = it.prev and s - 1 in AT_STATS_TAIL
                    if norm_prep:
                        att_mean_var_wait(t + 1)
                    if norm_b:
                        ffn_mean_var_wait(it.ffn_b)
                    if norm_a:
                        ffn_mean_var_wait(it.next_a)
                    if norm_tail:
                        dve.wait_ge(t_bn, 2 * (t - 1) + s // HALF + 1)
                    if it.cur:
                        row_maxima(t, s)
                    if norm_prep:
                        mean_var(att_bn, att_mv, TT, a_mv)
                    if norm_b:
                        ffn_mean_var(it.ffn_b)
                    if norm_a:
                        ffn_mean_var(it.next_a)
                    if norm_tail:
                        mean_var(tail_bn, tail_mv, 2, t_mv)
                    if it.cur and s % HB == HB - 1:
                        split_max(t, s // HB)
                    if 0 < s < HALF and it.ffn_a is not None:
                        ffn_piece(it.ffn_a, s - 1, x2[par], x3, stored=t - 2)
                    if s > HALF and it.ffn_b is not None:
                        ffn_piece(it.ffn_b, s - 1 - HALF, x0, x1[par], based=t + 1)
                    if it.prev:
                        if s - 1 == AT_MAX[3]:
                            copy_max(t - 1, 3)
                        for b, a in ((0, 0), (0, 1), (1, 0), (1, 1)):
                            if s - 1 == AT[f"CT{b}{a}"]:
                                context_norm(t - 1, b, a, it.misc[f"CT{b}{a}"])
                        if s in AT_STATS_TAIL:
                            tail_stats(t - 1, s // HALF)
                    if it.cur:
                        for hb in range(3):
                            if s - 1 == AT_MAX[hb]:
                                copy_max(t, hb)
                    if it.prep:
                        if s == AT_STATS_PREP:
                            att_stats(1 - par, first_ffn(t + 1))
                        if s - 1 == AT["LNT"]:
                            att_rest(t + 1)
                        if s - 1 == AT["Q"]:
                            qk_rest(t + 1, 0)
                        if s - 1 == AT["K"]:
                            qk_rest(t + 1, 1)
                    if it.ffn_b is not None and s == AT_STATS_B:
                        dve.wait_ge(s_x0, 16 * (t + 2))
                        ffn_stats(x0)
                    if it.next_a is not None and s == AT_STATS_A:
                        dve.wait_ge(s_x2, 2 * t)
                        ffn_stats(x2[1 - par])

            run(dve, steps)
            for s in range(16):
                ffn_piece(LAST_FFN, s, x2[(TILES - 1) % 2], x3, stored=TILES - 1)


NAMES = ["L0_attn_x", "L0_attn_Wq", "L0_attn_bq", "L0_attn_Wk", "L0_attn_bk", "L0_attn_Wv", "L0_attn_bv",
         "L0_attn_gamma", "L0_attn_beta", "L0_ffn_k0", "L0_ffn_k1", "L0_ffn_k2", "L0_ffn_s0", "L0_ffn_s1", "L0_ffn_s2"]


def kernel(**inputs):
    import concourse.bacc as bacc
    from concourse.bass_utils import run_bass_kernel_spmd

    nc = bacc.Bacc("TRN2", target_bir_lowering=False, num_devices=1)
    arrays, args = {}, []
    for name in NAMES:
        a = np.ascontiguousarray(inputs[name])
        if a.ndim == 0:
            a = a.reshape(1)
        arrays[name] = a
        args.append(nc.dram_tensor(name, a.shape, mybir.dt.from_np(a.dtype), kind="ExternalInput").ap())
    shape = inputs["L0_attn_x"].shape
    args.append(nc.dram_tensor("y", shape, F32, kind="ExternalOutput").ap())
    macaron_layer(nc, *args)
    result = run_bass_kernel_spmd(nc, [arrays], core_ids=[0])
    return result.results[0]["y"]
```

```python
import numpy as np
from contextlib import ExitStack

import concourse.bass as bass
from concourse import mybir
from concourse.alu_op_type import AluOpType as ALU

F32 = mybir.dt.float32
F16 = mybir.dt.float16
U8 = mybir.dt.uint8
ACT = mybir.ActivationFunctionType
AX = mybir.AxisListType
RMAX = bass.bass_isa.ReduceOp.max

P = 128
SEQ = 256
TILE = 512
TT = TILE // P
HEADS, HD = 16, 8
GROUPS, LANES = 4, 4
ROWS = 32
PARTS = 3
CTX_ROWS = ROWS // 2
V_COLS = ROWS + CTX_ROWS
UNITS = 32
HALF = 16
HB = 8
HIDDEN = 512
KC = HIDDEN // P
EPS = 1e-5
XN_SCALE = 2.0 ** 8
W0_UNIT = 0.5
W1_UNIT = 2.0 ** -8
Q_MAX = 2.0 ** 13
M_UNIT = 2.0 ** -14
FFN_OUT = 0.5 * 2 * 2 / (XN_SCALE * W0_UNIT / 2 * W1_UNIT)

PACE_ZERO = {5 + piece * 25 // 14: piece for piece in range(15)}
PACE_FIRST = {int(30 * ((piece - 1) / 13) ** 0.8): piece for piece in range(1, 15)}
PACE_SECOND = {4 + piece * 26 // 14: piece for piece in range(15)}
PACE_LAST = {3 + piece: piece for piece in range(15)}

MISC = [("CT0", 4), ("LNT", 9), ("Q", 12), ("K", 15), ("CT1", 18), ("V", 31)]
AT = dict(MISC)
AT_ZERO = {"LNT": 2, "Q": 4, "K": 6, "V": 8}
AT_CONTEXT_LAST = (0, 3, 5, 7, 8)
AT_LAST = {"CT0": 3, "CT1": 9}
AT_MAX = (10, 17, 25, 2)
PREP_USES = ("LNT", "Q", "K", "V")
Z_USES = 10
SPREADS = 2 * LANES * PARTS
WARM_UP = 16
AT_STATS_PREP, AT_STATS_B, AT_STATS_A = 6, 7, 26
AT_STATS_TAIL = (12, 21)
AT_STATS_TAIL_LAST, AT_STATS_A_LAST, AT_STATS_A_PACED = (8, 11), 15, 29

FFN_IN = {2: 0, 3: 1, 4: 2, 5: 3}
FFN_MID = ((6, 0, 2), (7, 2, 4), (8, 4, 8), (9, 8, 11), (10, 11, 14), (11, 14, 16))
FFN_MID_DONE = {7: 0, 8: 1, 10: 2, 11: 3}
FFN_RESIDUAL = 14


class Iteration:

    def __init__(self, t, par, cur=True, prev=True, prep=True, ffn_a=None, ffn_b=None,
                 next_a=None, misc_base=None, load=True, pace=None):
        self.t, self.par, self.cur, self.prev, self.prep = t, par, cur, prev, prep
        self.ffn_a, self.ffn_b = ffn_a, ffn_b
        self.pace = pace
        self.load = load
        self.next_a = next_a
        names = [n for n, _ in MISC if
                 (n in PREP_USES and prep) or (n in ("CT0", "CT1") and prev)]
        self.misc = {n: misc_base + i for i, n in enumerate(names)}


def macaron_layer(nc, x, wq, bq, wk, bk, wv, bv, gamma, beta, k0, k1, k2, s0, s1, s2, out):
    tokens = x.shape[0] * x.shape[1]
    TILES = tokens // TILE
    x_flat = x.rearrange("n s d -> (n s d)")
    out_flat = out.rearrange("n s d -> (n s d)")

    with ExitStack() as ctx:
        def sb(name, shape, dt=F32):
            return ctx.enter_context(nc.sbuf_tensor(name, shape, dt))

        def bank(name):
            return ctx.enter_context(nc.psum_tensor(name, [P, TILE], F32))

        def sem(name):
            return ctx.enter_context(nc.semaphore(name))

        ident = sb("ident", [P, P])
        ident16 = sb("ident16", [P, P], F16)
        lane_order = sb("lane_order", [P, P])
        k0_raw = sb("k0_raw", [P, 2, HIDDEN], U8)
        k1_raw = sb("k1_raw", [P, KC, HIDDEN], U8)
        k2_raw = sb("k2_raw", [P, KC, P], U8)
        w0 = sb("w0", [P, HIDDEN], F16)
        w0_diff = sb("w0_diff", [P, HIDDEN], F16)
        w1 = sb("w1", [P, KC, HIDDEN], F16)
        w2 = sb("w2", [P, KC, P], F16)
        s_raw = sb("s_raw", [P, 3])
        s_sign = sb("s_sign", [P, 2])
        s_tmp = sb("s_tmp", [P, 4])
        w0_scale = sb("w0_scale", [P, 1])
        w1_scale = sb("w1_scale", [P, 2])
        ffn_scale = sb("ffn_scale", [P, 1])
        w_raw = sb("w_raw", [P, 3, P])
        w_sq = sb("w_sq", [P, 3, P])
        w_fit = sb("w_fit", [P, 3, P])
        b_raw = sb("b_raw", [P, 3])
        b_abs = sb("b_abs", [P, 3])
        b_fit = sb("b_fit", [P, 3])
        w_norm = sb("w_norm", [P, 3])
        w_bound = sb("w_bound", [P, 3])
        w_most = sb("w_most", [P, 3])
        w_inv = sb("w_inv", [P, 3])
        w_factor = sb("w_factor", [P, 3])
        score_tmp = sb("score_tmp", [P, 1])
        score_scale = sb("score_scale", [P, 1])
        v_unscale = sb("v_unscale", [P, 1])
        wt_hi = sb("wt_hi", [P, 3, P], F16)
        wt_lo = sb("wt_lo", [P, 3, P], F16)
        gamma_b = sb("gamma_b", [P, P])
        beta_b = sb("beta_b", [P, P])
        bv_b = sb("bv_b", [P, P])
        minus_half = sb("minus_half", [P, TT])
        plus_half = sb("plus_half", [P, 3])
        eps = sb("eps", [P, TT])
        x0 = sb("x0", [P, TT, P])
        x1 = [sb(f"x1_{i}", [P, TT, P]) for i in range(2)]
        x2 = [sb(f"x2_{i}", [P, TT, P]) for i in range(2)]
        x3 = sb("x3", [P, TT, P])
        ffn_bn = sb("ffn_bn", [P, TT, 6])
        ffn_mv = sb("ffn_mv", [P, TT, 2])
        ffn_xc = sb("ffn_xc", [P, TT, P])
        ffn_ve = sb("ffn_ve", [P, TT])
        ffn_rs = sb("ffn_rs", [P, TT])
        ffn_xn = sb("ffn_xn", [P, TT, P])
        ffn_hi = sb("ffn_hi", [P, 9, TILE], F16)
        ffn_lo = sb("ffn_lo", [P, 9, TILE], F16)
        att_bn = sb("att_bn", [P, TT, 6])
        att_mv = sb("att_mv", [P, TT, 2])
        att_xc = sb("att_xc", [P, TT, P])
        att_ve = sb("att_ve", [P, TT])
        att_rs = sb("att_rs", [P, TT])
        att_xn = [sb(f"att_xn{i}", [P, TT, P]) for i in range(2)]
        att_hi = sb("att_hi", [P, TILE], F16)
        att_lo = sb("att_lo", [P, TILE], F16)
        qk_hi = [sb(f"{n}_hi", [P, TILE], F16) for n in "qk"]
        qk_lo = [sb(f"{n}_lo", [P, TILE], F16) for n in "qk"]
        q_rows = [sb(f"q_rows{i}", [P, GROUPS, TILE], F16) for i in range(2)]
        k_rows = [sb(f"k_rows{i}", [P, GROUPS, TILE], F16) for i in range(2)]
        v_cols = [sb(f"v_cols{i}", [P, TT, HEADS, V_COLS]) for i in range(2)]
        row_max = [sb(f"row_max{i}", [P, 2 * LANES, 2]) for i in range(2)]
        max_parts = sb("max_parts", [P, 2 * LANES, 2, 2], F16)
        max_rows = sb("max_rows", [4 * LANES, SEQ], F16)
        probs = [sb(f"probs{i}", [P, LANES, TILE]) for i in range(2)]
        ctx_t = sb("ctx_t", [P, GROUPS, SEQ])
        den = sb("den", [P, 2, HEADS])
        ctx_n = sb("ctx_n", [P, 2, P])
        att_y = sb("att_y", [P, 2, P])
        tail_bn = sb("tail_bn", [P, 2, 6])
        tail_mv = sb("tail_mv", [P, 2, 2])
        tail_xc = sb("tail_xc", [P, 2, P])
        tail_ve = sb("tail_ve", [P, 2])
        tail_rs = sb("tail_rs", [P, 2])
        tail_n = sb("tail_n", [P, 2, P])
        tail_g = sb("tail_g", [P, 2, P])
        xn_bv = [sb(f"xn_bv{i}", [P, TT, P]) for i in range(2)]
        x1_beta = [sb(f"x1_beta{i}", [P, TT, P]) for i in range(2)]

        ps_z = [bank(f"ps_z{i}") for i in range(2)]
        ps_s = [bank(f"ps_s{i}") for i in range(2)]
        ps_t = [bank(f"ps_t{i}") for i in range(2)]
        ps_c = bank("ps_c")
        ps_m = bank("ps_m")

        s_ffn_in = sem("ffn_params_loaded")
        s_proj_in = sem("projections_loaded")
        s_norm_in = sem("gamma_beta_bv_loaded")
        s_tile1 = sem("tile1_loaded")
        s_x0 = sem("x0_loaded")
        s_out = sem("out_stored")
        s_const = sem("consts_made")
        s_setd = sem("setup_vector")
        s_setp = sem("setup_pool")
        s_wt = sem("wt_transposed")
        s_wthi = sem("wt_hi_made")
        s_w1 = sem("w1_made")
        f_bn, f_mv, f_rs, f_xn = sem("ffn_bn_done"), sem("ffn_mv_done"), sem("ffn_rstd_steps"), sem("ffn_xn_done")
        z_full, z_hi, z_free = sem("z_full"), sem("z_hi_made"), sem("z_free")
        a_bn, a_mv, a_rs, a_xn = sem("att_bn_done"), sem("att_mv_done"), sem("att_rstd_steps"), sem("att_xn_done")
        m_full, m_hi, m_free = sem("misc_full"), sem("misc_hi_made"), sem("misc_free")
        mt_full, mt_free = sem("max_transposed"), sem("max_copied")
        s_spread = sem("rows_spread")
        s_full, s_max = sem("scores_full"), sem("max_done")
        s_mparts = sem("max_parts_made")
        s_mrows = sem("max_rows_placed")
        t_full, s_exp = sem("shifted_scores_full"), sem("exp_done")
        c_full, c_free = sem("context_full"), sem("context_copied")
        s_den = sem("den_inverted")
        s_y = sem("att_y_done")
        t_bn, t_mv, t_rs = sem("tail_bn_done"), sem("tail_mv_done"), sem("tail_rstd_steps")
        t_n = sem("tail_steps")
        s_x2 = sem("x2_done")
        s_base = sem("tail_base_done")

        def full(t, r):
            return Iteration(t, r, ffn_a=2 * t, ffn_b=2 * t + 1, next_a=2 * t + 2, misc_base=6 * t + 2)

        head = [Iteration(0, 0, prev=False, ffn_b=2, misc_base=4, load=False, pace=PACE_ZERO),
                Iteration(1, 1, ffn_b=3, next_a=4, misc_base=8)]
        LOOP_FROM, LOOP_TO = 2, TILES - 2
        T = TILES
        tail = [Iteration(T - 2, 0, ffn_a=2 * (T - 2), next_a=2 * (T - 2) + 1, misc_base=6 * (T - 2) + 2, pace=PACE_FIRST),
                Iteration(T - 1, 1, prep=False, ffn_a=2 * (T - 2) + 1, next_a=2 * (T - 2) + 2,
                          misc_base=6 * (T - 1) + 2, pace=PACE_SECOND),
                Iteration(T, 0, cur=False, prep=False, ffn_a=2 * (T - 2) + 2,
                          next_a=2 * (T - 2) + 3, misc_base=6 * (T - 1) + 4, pace=PACE_LAST)]
        LAST_FFN = 2 * T - 1
        assert (LOOP_TO - LOOP_FROM) % 2 == 0 and LOOP_FROM % 2 == 0

        def run(eng, steps):
            for it in head:
                steps(it)
            with eng.Fori(0, (LOOP_TO - LOOP_FROM) // 2) as pair:
                for r in range(2):
                    steps(full(pair * 2 + (LOOP_FROM + r), r))
            for it in tail:
                steps(it)

        CONST_IDENT, CONST_NORM, CONSTS = 4, 8, 14
        SETD_W0, SETD_FFN, SETD_SQUARES, SETD_BOUND, SETD_FIT, SETD_ALL = 7, 11, 13, 15, 19, 24
        AT_WT, AT_WT_HI, AT_WT_LO = 11, 12, 13
        FIRST = {3: "LNT", 4: "Q", 5: "K", 6: "V"}

        def first_ffn(tile):
            return tile if isinstance(tile, int) and tile <= 3 else 2 * tile - 3

        def at(it, name):
            return (AT_LAST if not it.cur else AT if it.prev else AT_ZERO)[name]

        def ffn_work(it, s):
            work = []
            if it.pace:
                f = it.ffn_b if it.ffn_a is None else it.ffn_a
                work = [(f, it.ffn_b is None, it.pace[s])] if s in it.pace else []
            elif s < HALF - 1 and it.ffn_a is not None:
                work = [(it.ffn_a, True, s)] if s else []
            elif s >= HALF and it.ffn_b is not None:
                work = [(it.ffn_b, False, s - HALF)] if HALF < s < UNITS - 1 else []
            if s == HALF - 1 and it.ffn_b is not None and not it.pace:
                work = [(it.ffn_b, False, 0)]
            if s == UNITS - 1 and it.next_a is not None and not it.pace:
                work = [(it.next_a, True, 0)]
            return work

        def ffn_rests(it, s):
            if s:
                return ffn_work(it, s - 1)
            return [] if it.ffn_a is None or it.pace and 0 in it.pace.values() else [(it.ffn_a, True, 0)]

        def softmax_units(it, s):
            if not it.cur:
                return it.t - 1, 1 - it.par, range(HALF + 2 * s, HALF + 2 * s + 2) if s < HALF // 2 else ()
            if s < HALF:
                return it.t - 1, 1 - it.par, (s + HALF,) if it.prev else ()
            return it.t, it.par, (s - HALF,)

        def contexts(it, s):
            if not it.cur:
                return it.t - 1, 1 - it.par, (AT_CONTEXT_LAST.index(s) + 3,) if s in AT_CONTEXT_LAST else ()
            if s <= HALF + 1:
                return it.t - 1, 1 - it.par, (s // LANES + 3,) if it.prev and s % LANES == 1 else ()
            return it.t, it.par, ((s - HALF - 5) // LANES,) if s in (21, 25, 29) else ()

        def unit(u):
            return u // HALF, u // LANES % GROUPS, u % LANES

        def softmax_lane(u):
            return (u + LANES // 2) % LANES

        def at_least(eng, s, n):
            if not isinstance(n, int) or n > 0:
                eng.wait_ge(s, n)

        block = ctx.enter_context(nc.Block())

        @block.sync
        def _(sp):
            def start_of(t):
                return t * (TILE * P) if isinstance(t, int) else sp.snap(t * (TILE * P))

            def tile_rows(flat, start):
                return flat[bass.ds(start, TILE * P)].rearrange("(b p a d) -> p b a d", b=2, p=P, a=2)

            def load_x(start):
                sp.dma_start(x0[:].rearrange("p (b a) d -> p b a d", b=2), tile_rows(x_flat, start)).then_inc(s_x0, 16)

            def store_x3(start):
                sp.dma_start(tile_rows(out_flat, start), x3[:].rearrange("p (b a) d -> p b a d", b=2)).then_inc(s_out, 16)

            def spread(par, lo, hi):
                n = 0
                for w, rows in ((0, q_rows), (1, k_rows)):
                    for part in range(PARTS):
                        src = (qk_lo if part == (2, 1)[w] else qk_hi)[w]
                        for j in range(LANES):
                            if lo <= n < hi:
                                sp.dma_start(rows[par][ROWS * j + HD * part:ROWS * j + HD * (part + 1), :, :],
                                             src[ROWS * j:ROWS * (j + 1), :]).then_inc(s_spread, 16)
                            n += 1

            def place_max(t, par, hb):
                sp.wait_ge(mt_free, 4 * t + hb + 1)
                b, g0 = hb // 2, 2 * (hb % 2)
                for j in range(LANES):
                    r = ROWS * j + HD * PARTS
                    sp.dma_start(q_rows[par][r:r + 2, g0:g0 + 2, b * SEQ:(b + 1) * SEQ],
                                 max_rows[4 * j:4 * j + 4, :]).then_inc(s_mrows, 16)

            load_x(start_of(0))
            for i, scale in enumerate((s0, s1, s2)):
                sp.dma_start(s_raw[:, i:i + 1], scale.partition_broadcast(P)).then_inc(s_ffn_in, 16)
            for dst, src in ((k0_raw, k0), (k1_raw, k1), (k2_raw, k2)):
                sp.dma_start(dst[:], src.rearrange("(c p) n -> p c n", p=P)).then_inc(s_ffn_in, 16)
            for i, w in enumerate((wq, wk, wv)):
                sp.dma_start(w_raw[:, i, :], w).then_inc(s_proj_in, 16)
            for i, b in enumerate((bq, bk, bv)):
                sp.dma_start(b_raw[:, i:i + 1], b.rearrange("(n a) -> n a", a=1)).then_inc(s_proj_in, 16)
            sp.dma_start(x3[:].rearrange("p (b a) d -> p b a d", b=2), tile_rows(x_flat, start_of(1))).then_inc(s_tile1, 16)
            for dst, src in ((gamma_b, gamma), (beta_b, beta), (bv_b, bv)):
                sp.dma_start(dst[:], src.partition_broadcast(P)).then_inc(s_norm_in, 16)
            sp.wait_ge(z_free, Z_USES)
            load_x(start_of(2))
            sp.wait_ge(m_free, 2)
            spread(0, 0, SPREADS // 2)
            sp.wait_ge(m_free, 3)
            sp.wait_ge(s_const, CONSTS)
            spread(0, SPREADS // 2, SPREADS)

            def steps(it):
                t, par = it.t, it.par
                if it.ffn_b is not None and it.load:
                    start = start_of(t + 2)
                    sp.wait_ge(z_free, Z_USES * (first_ffn(t + 1) + 1))
                    load_x(start)
                if it.prev:
                    place_max(t - 1, 1 - par, 3)
                if it.cur and it.prev:
                    place_max(t, par, 0)
                if it.ffn_a is not None and not it.pace:
                    start = start_of(t - 2)
                    sp.wait_ge(z_free, Z_USES * it.ffn_a + Z_USES)
                    store_x3(start)
                if it.prep:
                    sp.wait_ge(m_free, it.misc["K"] + 1)
                    if it.prev:
                        sp.wait_ge(t_full, UNITS * t + 1)
                    spread(1 - par, 0, 6)
                if it.cur and not it.prev:
                    place_max(t, par, 0)
                    spread(1 - par, 6, 14)
                if it.cur:
                    place_max(t, par, 1)
                if it.prep:
                    spread(1 - par, 6 if it.prev else 14, SPREADS)
                if it.cur:
                    place_max(t, par, 2)
                if it.ffn_a is not None and it.pace:
                    start = start_of(t - 2)
                    sp.wait_ge(z_free, Z_USES * it.ffn_a + Z_USES)
                    store_x3(start)

            run(sp, steps)
            sp.wait_ge(z_free, Z_USES * (LAST_FFN + 1))
            store_x3(start_of(TILES - 1))
            sp.wait_ge(s_out, 16 * TILES)

        @block.gpsimd
        def _(pool):
            g = nc.gpsimd
            g.memset(ident[:], 0.0).then_inc(s_const, 1)
            g.memset(ident16[:], 0.0).then_inc(s_const, 1)
            pool.wait_ge(s_const, 2)
            for m in (ident, ident16):
                g.affine_select(out=m[:], in_=m[:], compare_op=ALU.not_equal, fill=1.0, base=0,
                                pattern=[[-1, P]], channel_multiplier=1).then_inc(s_const, 1)
            g.memset(minus_half[:], -0.5).then_inc(s_const, 1)
            g.memset(plus_half[:], 0.5).then_inc(s_const, 1)
            g.memset(eps[:], EPS).then_inc(s_const, 1)
            pool.wait_ge(s_const, CONST_IDENT)
            for j in range(LANES):
                last = g.tensor_copy(lane_order[:].rearrange("p (j i x e) -> p j i x e", j=LANES, x=2, e=2)[:, j],
                                     ident[:].rearrange("p (x j e i) -> p j i x e", x=2, j=LANES, e=2)[:, j])
            last.then_inc(s_const, 1)

            def normalize(dst, src, mv, xc, ve, rs, n, steps_done, k, done):
                shape = [P, n, P]
                g.tensor_tensor(ve[:], mv[:, :, 1], eps[:, 0:n], ALU.add).then_inc(steps_done, 1)
                g.tensor_tensor(xc[:], src, mv[:, :, 0:1].broadcast_to(shape), ALU.subtract)
                pool.wait_ge(steps_done, k + 1)
                g.tensor_tensor(rs[:], ve[:], minus_half[:, 0:n], ALU.pow).then_inc(steps_done, 1)
                pool.wait_ge(steps_done, k + 2)
                g.tensor_tensor(dst, xc[:], rs[:].unsqueeze(2).broadcast_to(shape), ALU.mult).then_inc(done, 1)

            def ffn_norm(f, src):
                at_least(pool, z_full, Z_USES * f - (Z_USES - 1))
                pool.wait_ge(f_mv, f + 1)
                normalize(ffn_xn[:], src[:], ffn_mv, ffn_xc, ffn_ve, ffn_rs, TT, f_rs, 2 * f, f_xn)

            def att_norm(t, par):
                pool.wait_ge(a_mv, t + 1)
                normalize(att_xn[par][:], x1[par][:], att_mv, att_xc, att_ve, att_rs, TT, a_rs, 2 * t, a_xn)

            def tail_y(t, b, par, use):
                pool.wait_ge(s_base, t + 1)
                pool.wait_ge(m_free, use + 1)
                g.tensor_tensor(att_y[:], ctx_n[:], xn_bv[par][:, 2 * b:2 * b + 2, :], ALU.add).then_inc(s_y, 1)

            def tail_norm(t, b, par):
                n = 2 * t + b
                pool.wait_ge(t_mv, n + 1)
                normalize(tail_n[:], att_y[:], tail_mv, tail_xc, tail_ve, tail_rs, 2, t_rs, 2 * n, t_n)
                pool.wait_ge(t_n, 2 * n + 1)
                g.tensor_tensor(tail_g[:], tail_n[:], gamma_b[:].unsqueeze(1).broadcast_to([P, 2, P]),
                                ALU.mult).then_inc(t_n, 1)
                pool.wait_ge(t_n, 2 * n + 2)
                g.tensor_tensor(x2[par][:, 2 * b:2 * b + 2, :], tail_g[:], x1_beta[par][:, 2 * b:2 * b + 2, :],
                                ALU.add).then_inc(s_x2, 1)

            def tail_base(t, par):
                at_least(pool, s_x2, 2 * (t - 1))
                g.tensor_tensor(x1_beta[par][:], x1[par][:], beta_b[:].unsqueeze(1).broadcast_to([P, TT, P]), ALU.add)
                g.tensor_tensor(xn_bv[par][:], att_xn[par][:], bv_b[:].unsqueeze(1).broadcast_to([P, TT, P]),
                                ALU.add).then_inc(s_base, 1)

            pool.wait_ge(s_const, CONST_NORM)
            ffn_norm(0, x0)
            pool.wait_ge(s_setd, SETD_SQUARES)
            g.tensor_tensor(w_norm[:], w_bound[:], plus_half[:], ALU.pow).then_inc(s_setp, 1)
            pool.wait_ge(s_setd, SETD_BOUND)
            g.partition_all_reduce(w_most[:], w_inv[:], P, RMAX).then_inc(s_setp, 1)
            for i in range(2):
                g.memset(k_rows[i][:], -1.0 / M_UNIT).then_inc(s_const, 1)
                g.memset(v_cols[i][:], 0.0).then_inc(s_const, 1)
            pool.wait_ge(s_const, CONSTS - 2)
            for i in range(2):
                g.memset(v_cols[i][:, :, :, HD:HD + 1], 1.0).then_inc(s_const, 1)
            ffn_norm(1, x3)
            att_norm(0, 0)
            pool.wait_ge(s_norm_in, 16 * 3)

            def steps(it):
                t, par = it.t, it.par
                if it.prep:
                    att_norm(t + 1, 1 - par)
                if it.ffn_b is not None:
                    ffn_norm(it.ffn_b, x0)
                if it.prev:
                    tail_y(t - 1, 0, 1 - par, it.misc["CT0"])
                    tail_norm(t - 1, 0, 1 - par)
                if it.cur:
                    tail_base(t, par)
                if it.prev:
                    tail_y(t - 1, 1, 1 - par, it.misc["CT1"])
                    tail_norm(t - 1, 1, 1 - par)
                if it.next_a is not None:
                    ffn_norm(it.next_a, x2[1 - par])

            run(pool, steps)

        @block.tensor
        def _(pe):
            def bank_of(use):
                return ps_z[use % 2]

            def ffn_transpose(f):
                at_least(pe, z_free, Z_USES * f - 1)
                pe.wait_ge(f_xn, f + 1)
                for i in range(TT):
                    last = pe.transpose(bank_of(0)[:, i * P:(i + 1) * P], ffn_xn[:, i, :], ident[:])
                last.then_inc(z_full, 1)

            def ffn_in(f, m):
                pe.wait_ge(z_free, Z_USES * f + 1 + max(0, m - 1))
                o = bank_of(1 + m)
                pe.matmul(o[:], w0[:, m * P:(m + 1) * P], ffn_hi[:, 0, :], start=True, stop=False)
                pe.matmul(o[:], w0[:, m * P:(m + 1) * P], ffn_lo[:, 0, :], start=False, stop=True).then_inc(z_full, 1)

            def ffn_mid(f, n):
                m, k = n // KC, n % KC
                o = bank_of(5 + m)
                pe.wait_ge(z_free, Z_USES * f + max(2 + k, 4 + m))
                w = w1[:, k, m * P:(m + 1) * P]
                pe.matmul(o[:], w, ffn_hi[:, 1 + k, :], start=(k == 0), stop=False)
                last = pe.matmul(o[:], w, ffn_lo[:, 1 + k, :], start=False, stop=(k == KC - 1))
                if k == KC - 1:
                    last.then_inc(z_full, 1)

            def ffn_out(f, i, k):
                o = bank_of(9)[:, i * P:(i + 1) * P]
                if i == 0:
                    pe.wait_ge(z_free, Z_USES * f + max(6 + k, 8))
                pe.matmul(o, ffn_hi[:, 5 + k, i * P:(i + 1) * P], w2[:, k, :], start=(i == 0 and k == 0),
                          stop=False)
                last = pe.matmul(o, ffn_lo[:, 5 + k, i * P:(i + 1) * P], w2[:, k, :], start=False,
                                 stop=(i == TT - 1 and k == KC - 1))
                if i == TT - 1 and k == KC - 1:
                    last.then_inc(z_full, 1)

            def ffn_piece(f, s):
                if s == 0:
                    ffn_transpose(f)
                elif s in FFN_IN:
                    ffn_in(f, FFN_IN[s])
                for at, lo, hi in FFN_MID:
                    if s == at:
                        for n in range(lo, hi):
                            ffn_mid(f, n)
                for k in {12: (0, 1), 13: (2,), 14: (3,)}.get(s, ()):
                    for i in range(TT):
                        ffn_out(f, i, k)

            def misc_wait(use):
                at_least(pe, m_free, use)

            def att_transpose(t, par, use):
                misc_wait(use)
                pe.wait_ge(a_xn, t + 1)
                for i in range(TT):
                    last = pe.transpose(ps_m[:, i * P:(i + 1) * P], att_xn[par][:, i, :], ident[:])
                last.then_inc(m_full, 1)

            def project(w, use):
                misc_wait(use)
                n = 0
                for ww in (wt_hi, wt_lo):
                    for xx in (att_hi, att_lo):
                        last = pe.matmul(ps_m[:], ww[:, w, :], xx[:], start=(n == 0), stop=(n == 3))
                        n += 1
                last.then_inc(m_full, 1)

            def project_v(use):
                misc_wait(use)
                for i in range(TT):
                    n = 0
                    for xx in (att_hi, att_lo):
                        for ww in (wt_hi, wt_lo):
                            last = pe.matmul(ps_m[:, i * P:(i + 1) * P], xx[:, i * P:(i + 1) * P], ww[:, 2, :],
                                             start=(n == 0), stop=(n == 3))
                            n += 1
                last.then_inc(m_full, 1)

            def scores(t, par, u):
                b, g, j = unit(u)
                n = UNITS * t + u
                if u == 0:
                    pe.wait_ge(s_spread, 16 * SPREADS * (t + 1))
                at_least(pe, s_max, n - 1)
                r = slice(ROWS * j, ROWS * j + HD * PARTS)
                for a in range(2):
                    c = b * SEQ + a * P
                    last = pe.matmul(ps_s[u % 2][:, a * SEQ:(a + 1) * SEQ], q_rows[par][r, g, c:c + P],
                                     k_rows[par][r, g, b * SEQ:(b + 1) * SEQ], start=True, stop=True)
                last.then_inc(s_full, 1)

            def shifted(t, par, u):
                b, g, _ = unit(u)
                j = softmax_lane(u)
                n = UNITS * t + u
                if u % HB == 0:
                    pe.wait_ge(s_mrows, 64 * (4 * t + u // HB + 1))
                at_least(pe, s_exp, n - 1)
                r = slice(ROWS * j, ROWS * j + HD * PARTS + 2)
                for a in range(2):
                    c = b * SEQ + a * P
                    last = pe.matmul(ps_t[u % 2][:, a * SEQ:(a + 1) * SEQ], k_rows[par][r, g, c:c + P],
                                     q_rows[par][r, g, b * SEQ:(b + 1) * SEQ], start=True, stop=True)
                last.then_inc(t_full, 1)

            def context(t, par, grp):
                b, g = grp // GROUPS, grp % GROUPS
                n = 2 * GROUPS * t + grp
                pe.wait_ge(s_exp, LANES * n + LANES)
                if g % 2 == 0:
                    at_least(pe, c_free, GROUPS * t + grp // 2)
                    last_tile = isinstance(t, int) and t == TILES - 1
                    pe.wait_ge(mt_free, 4 * t + (min(4, 2 + grp // 2) if last_tile else 2 + grp // 2))
                for a in range(2):
                    v = v_cols[par][:, 2 * b + a].rearrange("p h c -> p (h c)")
                    for j in range(LANES):
                        col = V_COLS * (2 * LANES * (g // 2) + 2 * j + g % 2) - CTX_ROWS * (g % 2)
                        last = pe.matmul(ps_c[ROWS * j:ROWS * (j + 1), 0:SEQ], v[:, col:col + ROWS],
                                         probs[grp % 2][:, j, a * SEQ:(a + 1) * SEQ],
                                         start=(a == 0 and g % 2 == 0), stop=(a == 1 and g % 2 == 1))
                last.then_inc(c_full, 1)

            def context_transpose(t, b, use):
                misc_wait(use)
                pe.wait_ge(c_free, GROUPS * t + 2 * (b + 1))
                for a in range(2):
                    for pair in range(2):
                        c = (2 * a + pair) * P
                        last = pe.transpose(ps_m[:, c:c + P], ctx_t[:, 2 * b + pair, a * P:(a + 1) * P], ident[:])
                last.then_inc(m_full, 1)

            def max_transpose(t, hb):
                at_least(pe, c_free, GROUPS * t + hb - 1)
                at_least(pe, mt_free, 4 * t + hb)
                pe.wait_ge(s_mparts, 2 * (4 * t + hb + 1))
                for a in range(2):
                    last = pe.transpose(ps_c[:].bitcast(F16)[0:4 * LANES, 2 * SEQ + a * P:2 * SEQ + (a + 1) * P],
                                        max_parts[:, a * LANES:(a + 1) * LANES].rearrange("p j c g -> p (j c g)"),
                                        ident16[:])
                last.then_inc(mt_full, 1)

            def project_weights():
                pe.wait_ge(s_setd, SETD_FIT)
                for i, order in enumerate((lane_order, lane_order, ident)):
                    pe.matmul(ps_c[:, i * P:(i + 1) * P], w_fit[:, i, :], order[:], start=True, stop=True)
                for i in range(2):
                    last = pe.matmul(ps_c[:, 3 * P + i:3 * P + i + 1], lane_order[:], b_raw[:, i:i + 1],
                                     start=True, stop=True)
                last.then_inc(s_wt, 1)

            pe.wait_ge(s_const, CONST_NORM)
            for i in range(WARM_UP):
                pe.matmul(ps_s[0][:], ident16[:], ident16[:].unsqueeze(1).broadcast_to([P, TT, P]), start=True, stop=True)
            for s in range(16):
                if s == 1:
                    pe.wait_ge(s_setd, SETD_FFN)
                    pe.wait_ge(s_w1, 1)
                ffn_piece(0, s)
                if s == AT_WT:
                    project_weights()
            pe.wait_ge(s_setd, SETD_ALL)
            for s in range(16):
                ffn_piece(1, s)
                what = FIRST.get(s)
                if what == "LNT":
                    att_transpose(0, 0, 0)
                elif what == "Q":
                    project(0, 1)
                elif what == "K":
                    project(1, 2)
                elif what == "V":
                    project_v(3)

            def steps(it):
                t, par = it.t, it.par
                for s in range(UNITS):
                    if it.cur:
                        scores(t, par, s)
                    tile, parity, units = softmax_units(it, s)
                    for u in units:
                        shifted(tile, parity, u)
                    tile, parity, groups = contexts(it, s)
                    for g in groups:
                        context(tile, parity, g)
                    for f, _, piece in ffn_work(it, s):
                        ffn_piece(f, piece)
                    if it.prev:
                        if s == (AT_MAX[3] if it.cur else 1):
                            max_transpose(t - 1, 3)
                        for b in range(2):
                            if s == at(it, f"CT{b}"):
                                context_transpose(t - 1, b, it.misc[f"CT{b}"])
                    if it.cur:
                        for hb in range(3):
                            if s == AT_MAX[hb]:
                                max_transpose(t, hb)
                    if it.prep:
                        if s == at(it, "LNT"):
                            att_transpose(t + 1, 1 - par, it.misc["LNT"])
                        if s == at(it, "Q"):
                            project(0, it.misc["Q"])
                        if s == at(it, "K"):
                            project(1, it.misc["K"])
                        if s == at(it, "V"):
                            project_v(it.misc["V"])

            run(pe, steps)
            for s in range(16):
                ffn_piece(LAST_FFN, s)

        @block.scalar
        def _(act):
            a_ = nc.scalar

            def z_split(f, use):
                act.wait_ge(z_full, Z_USES * f + use + 1)
                a_.activation(ffn_hi[:, use, :], ps_z[use % 2][:], ACT.Relu if use else ACT.Copy,
                              scale=1.0 if use else XN_SCALE).then_inc(z_hi, 1)

            def ffn_piece(f, s):
                if s == 0:
                    z_split(f, 0)
                elif s in FFN_IN:
                    z_split(f, 1 + FFN_IN[s])
                elif s in FFN_MID_DONE:
                    z_split(f, 5 + FFN_MID_DONE[s])

            def att_split(use):
                act.wait_ge(m_full, use + 1)
                a_.activation(att_hi[:], ps_m[:], ACT.Copy, scale=XN_SCALE).then_inc(m_hi, 1)

            def qk_split(w, use):
                act.wait_ge(m_full, use + 1)
                a_.activation(qk_hi[w][:], ps_m[:], ACT.Identity, bias=b_fit[:, w:w + 1]).then_inc(m_hi, 1)

            def v_copy(t, par, use):
                act.wait_ge(m_full, use + 1)
                at_least(act, c_full, 2 * GROUPS * (t - 1))
                a_.activation(v_cols[par][:].rearrange("p t h c -> p (t h) c")[:, :, 0:HD],
                              ps_m[:].rearrange("p (n i) -> p n i", i=HD), ACT.Copy,
                              scale=v_unscale[:, 0:1]).then_inc(m_free, 1)

            def exps(t, u):
                n = UNITS * t + u
                grp = u // LANES
                act.wait_ge(t_full, n + 1)
                if u % LANES == 0:
                    at_least(act, c_full, 2 * GROUPS * t + grp - 1)
                a_.activation(probs[grp % 2][:, softmax_lane(u), :], ps_t[u % 2][:], ACT.Exp,
                              scale=score_scale[:, 0:1]).then_inc(s_exp, 1)

            def copy_max(t, hb):
                act.wait_ge(mt_full, 4 * t + hb + 1)
                at_least(act, s_mrows, 64 * (4 * t + hb))
                a_.activation(max_rows[:], ps_c[:].bitcast(F16)[0:4 * LANES, 2 * SEQ:3 * SEQ], ACT.Copy).then_inc(mt_free, 1)

            def context_copy(t, grp):
                if grp % 2:
                    act.wait_ge(c_full, 2 * GROUPS * t + grp + 1)
                    a_.activation(ctx_t[:, grp // 2, :], ps_c[:, 0:SEQ], ACT.Copy).then_inc(c_free, 1)

            act.wait_ge(s_setd, SETD_W0)
            a_.activation(w1[:], k1_raw[:], ACT.Identity, bias=w1_scale[:, 1:2], scale=w1_scale[:, 0:1]).then_inc(s_w1, 1)
            for s in range(16):
                ffn_piece(0, s)
                if s == AT_WT_HI:
                    act.wait_ge(s_wt, 1)
                    a_.activation(wt_hi[:].rearrange("p i n -> p (i n)"), ps_c[:, 0:3 * P], ACT.Copy).then_inc(s_wthi, 1)
            act.wait_ge(s_setd, SETD_ALL)
            for s in range(16):
                ffn_piece(1, s)
                what = FIRST.get(s)
                if what == "LNT":
                    att_split(0)
                elif what == "Q":
                    qk_split(0, 1)
                elif what == "K":
                    qk_split(1, 2)
                elif what == "V":
                    act.wait_ge(s_const, CONSTS)
                    v_copy(0, 0, 3)

            def steps(it):
                t, par = it.t, it.par
                for s in range(UNITS):
                    tile, _, units = softmax_units(it, s)
                    for u in units:
                        exps(tile, u)
                    for f, _, piece in ffn_work(it, s):
                        ffn_piece(f, piece)
                    if it.prev and s - 1 == (AT_MAX[3] if it.cur else 1):
                        copy_max(t - 1, 3)
                    if it.cur and s - 1 in AT_MAX[:3]:
                        copy_max(t, AT_MAX.index(s - 1))
                    tile, _, groups = contexts(it, s)
                    for g in groups:
                        context_copy(tile, g)
                    if it.prep:
                        if s == at(it, "LNT"):
                            att_split(it.misc["LNT"])
                        if s == at(it, "Q"):
                            qk_split(0, it.misc["Q"])
                        if s == at(it, "K"):
                            qk_split(1, it.misc["K"])
                        if s == at(it, "V"):
                            v_copy(t + 1, 1 - par, it.misc["V"])

            run(act, steps)
            for s in range(16):
                ffn_piece(LAST_FFN, s)

        @block.vector
        def _(dve):
            v = nc.vector
            done = [0]

            def step(ins):
                done[0] += 1
                ins.then_inc(s_setd, 1)

            def so_far():
                dve.wait_ge(s_setd, done[0])

            def setup_ffn():
                dve.wait_ge(s_ffn_in, 16 * 6)
                step(v.tensor_scalar(s_tmp[:, 0:2], s_raw[:, 0:2], 0.0, None, ALU.is_ge))
                so_far()
                step(v.tensor_scalar(s_sign[:], s_tmp[:, 0:2], 2.0, -1.0, ALU.mult, ALU.add))
                so_far()
                step(v.tensor_scalar(w0_scale[:], s_sign[:, 0:1], W0_UNIT, None, ALU.mult))
                step(v.tensor_scalar(w1_scale[:, 0:1], s_sign[:, 1:2], 2 * W1_UNIT, None, ALU.mult))
                step(v.tensor_scalar(w1_scale[:, 1:2], s_sign[:, 1:2], -W1_UNIT, None, ALU.mult))
                step(v.tensor_tensor(s_tmp[:, 2:4], s_raw[:, 0:2], s_sign[:], ALU.mult))
                step(v.tensor_tensor(w0_diff[:], k0_raw[:, 0, :], k0_raw[:, 1, :], ALU.subtract))
                so_far()
                assert done[0] == SETD_W0
                step(v.tensor_scalar(w0[:], w0_diff[:], w0_scale[:, 0:1], None, ALU.mult))
                step(v.tensor_scalar(score_tmp[:], s_tmp[:, 2:3], s_tmp[:, 3:4], FFN_OUT, ALU.mult, ALU.mult))
                step(v.tensor_scalar(w2[:], k2_raw[:], 2.0, -1.0, ALU.mult, ALU.add))
                so_far()
                step(v.tensor_tensor(ffn_scale[:], score_tmp[:], s_raw[:, 2:3], ALU.mult))
                assert done[0] == SETD_FFN

            def setup_squares():
                dve.wait_ge(s_proj_in, 16 * 6)
                step(v.tensor_tensor(w_sq[:], w_raw[:], w_raw[:], ALU.mult))
                so_far()
                step(v.tensor_reduce(w_bound[:], w_sq[:], AX.X, ALU.add))
                assert done[0] == SETD_SQUARES

            def setup_bound():
                step(v.scalar_tensor_tensor(out=b_abs[:], in0=b_raw[:], scalar=-1.0, in1=b_raw[:], op0=ALU.mult, op1=ALU.max))
                so_far()
                dve.wait_ge(s_setp, 1)
                step(v.scalar_tensor_tensor(out=w_inv[:], in0=w_norm[:], scalar=float(P) ** 0.5, in1=b_abs[:],
                                            op0=ALU.mult, op1=ALU.add))
                assert done[0] == SETD_BOUND

            def setup_fit():
                dve.wait_ge(s_setp, 2)
                step(v.tensor_scalar(w_norm[:], w_most[:], 1e-30, None, ALU.max))
                so_far()
                step(v.reciprocal(w_inv[:], w_norm[:]))
                so_far()
                step(v.tensor_scalar(w_factor[:], w_inv[:], Q_MAX, None, ALU.mult))
                so_far()
                for i in range(3):
                    last = v.tensor_scalar(w_fit[:, i, :], w_raw[:, i, :], w_factor[:, i:i + 1], 1.0 / XN_SCALE,
                                           ALU.mult, ALU.mult)
                step(last)
                assert done[0] == SETD_FIT

            def setup_projections():
                step(v.tensor_scalar(score_tmp[:], w_norm[:, 0:1], w_norm[:, 1:2], Q_MAX ** -2, ALU.mult, ALU.mult))
                so_far()
                step(v.tensor_scalar(score_scale[:], score_tmp[:], float(1.0 / np.sqrt(HD)), None, ALU.mult))
                step(v.tensor_scalar(v_unscale[:], w_norm[:, 2:3], 1.0 / Q_MAX, None, ALU.mult))
                dve.wait_ge(s_wthi, 1)
                step(v.tensor_tensor(b_fit[:, 0:2], ps_c[:, 3 * P:3 * P + 2], w_factor[:, 0:2], ALU.mult))
                step(v.tensor_tensor(wt_lo[:].rearrange("p i n -> p (i n)"), ps_c[:, 0:3 * P],
                                     wt_hi[:].rearrange("p i n -> p (i n)"), ALU.subtract))
                assert done[0] == SETD_ALL
                so_far()

            def stats(src, bn, n, bn_done):
                for i in range(n):
                    last = v.bn_stats(bn[:, i, :], src[:, i, :])
                last.then_inc(bn_done, 1)

            def mean_var(bn, mv, n, mv_done):
                for i in range(n):
                    last = v.bn_aggr(mv[:, i, :], bn[:, i, :])
                last.then_inc(mv_done, 1)

            def ffn_stats(src):
                stats(src, ffn_bn, TT, f_bn)

            def ffn_mean_var(f):
                mean_var(ffn_bn, ffn_mv, TT, f_mv)

            def ffn_mean_var_wait(f):
                at_least(dve, f_xn, f)
                dve.wait_ge(f_bn, f + 1)

            def z_rest(f, use):
                dve.wait_ge(z_hi, 9 * f + use + 1)
                if use:
                    v.scalar_tensor_tensor(out=ffn_lo[:, use, :], in0=ps_z[use % 2][:], scalar=0.0,
                                           in1=ffn_hi[:, use, :], op0=ALU.max, op1=ALU.subtract).then_inc(z_free, 1)
                else:
                    v.scalar_tensor_tensor(out=ffn_lo[:, 0, :], in0=ps_z[0][:], scalar=XN_SCALE,
                                           in1=ffn_hi[:, 0, :], op0=ALU.mult, op1=ALU.subtract).then_inc(z_free, 1)

            def ffn_residual(f, src, dst, stored=None, based=None):
                dve.wait_ge(z_full, Z_USES * f + Z_USES)
                if based is not None:
                    dve.wait_ge(s_base, based)
                if stored is not None:
                    at_least(dve, s_out, 16 * stored)
                v.scalar_tensor_tensor(out=dst[:].rearrange("p t d -> p (t d)"), in0=ps_z[1][:],
                                       scalar=ffn_scale[:, 0:1], in1=src[:].rearrange("p t d -> p (t d)"),
                                       op0=ALU.mult, op1=ALU.add).then_inc(z_free, 1)

            def ffn_piece(f, s, src, dst, stored=None, based=None):
                if s == 0:
                    z_rest(f, 0)
                elif s in FFN_IN:
                    z_rest(f, 1 + FFN_IN[s])
                elif s in FFN_MID_DONE:
                    z_rest(f, 5 + FFN_MID_DONE[s])
                elif s == FFN_RESIDUAL:
                    ffn_residual(f, src, dst, stored, based)

            def att_stats(par, f):
                dve.wait_ge(z_free, Z_USES * (f + 1))
                stats(x1[par], att_bn, TT, a_bn)

            def att_mean_var_wait(t):
                at_least(dve, a_xn, t)
                dve.wait_ge(a_bn, t + 1)

            def att_rest(t):
                dve.wait_ge(m_hi, 3 * t + 1)
                v.scalar_tensor_tensor(out=att_lo[:], in0=ps_m[:], scalar=XN_SCALE, in1=att_hi[:],
                                       op0=ALU.mult, op1=ALU.subtract).then_inc(m_free, 1)

            def qk_rest(t, w):
                dve.wait_ge(m_hi, 3 * t + 2 + w)
                v.scalar_tensor_tensor(out=qk_lo[w][:], in0=ps_m[:], scalar=b_fit[:, w:w + 1], in1=qk_hi[w][:],
                                       op0=ALU.add, op1=ALU.subtract).then_inc(m_free, 1)

            def row_maxima(t, u):
                b, g, j = unit(u)
                dve.wait_ge(s_full, UNITS * t + u + 1)
                if u % HB == 0:
                    at_least(dve, s_mparts, 2 * (4 * t + u // HB - 1))
                v.tensor_reduce(row_max[u // HB % 2][:, j::LANES, g % 2],
                                ps_s[u % 2][:].rearrange("p (a k) -> p a k", a=2), AX.X, ALU.max).then_inc(s_max, 1)

            def max_hi(t, hb):
                dve.wait_ge(s_max, UNITS * t + HB * (hb + 1))
                v.tensor_scalar(max_parts[:, :, 0, :], row_max[hb % 2][:], M_UNIT, None, ALU.mult).then_inc(s_mparts, 1)

            def max_lo(t, hb):
                dve.wait_ge(s_mparts, 2 * (4 * t + hb) + 1)
                v.scalar_tensor_tensor(out=max_parts[:, :, 1, :], in0=row_max[hb % 2][:], scalar=M_UNIT,
                                       in1=max_parts[:, :, 0, :], op0=ALU.mult, op1=ALU.subtract).then_inc(s_mparts, 1)

            def contexts_by_head():
                return ps_m[:].rearrange("p (a h r) -> p a h r", a=2, r=CTX_ROWS)

            def context_den(t, b, use):
                dve.wait_ge(m_full, use + 1)
                v.reciprocal(den[:], contexts_by_head()[:, :, :, HD]).then_inc(s_den, 1)

            def context_norm(t, b):
                dve.wait_ge(s_den, 2 * t + b + 1)
                at_least(dve, s_y, 2 * t + b)
                v.tensor_tensor(ctx_n[:].rearrange("p a (h i) -> p a h i", i=HD), contexts_by_head()[:, :, :, 0:HD],
                                den[:].unsqueeze(3).broadcast_to([P, 2, HEADS, HD]), ALU.mult).then_inc(m_free, 1)

            def tail_stats(t, b):
                dve.wait_ge(s_y, 2 * t + b + 1)
                stats(att_y, tail_bn, 2, t_bn)

            dve.wait_ge(s_x0, 16)
            ffn_stats(x0)
            ffn_mean_var_wait(0)
            ffn_mean_var(0)
            setup_ffn()
            for s in range(16):
                ffn_piece(0, s, x0, x1[0])
                if s == 0:
                    setup_squares()
                elif s == 2:
                    setup_bound()
                elif s == 5:
                    setup_fit()
                elif s == 7:
                    dve.wait_ge(s_tile1, 16)
                    ffn_stats(x3)
                elif s == 8:
                    ffn_mean_var_wait(1)
                    ffn_mean_var(1)
                elif s == AT_WT_LO:
                    setup_projections()
            att_stats(0, 0)
            att_mean_var_wait(0)
            mean_var(att_bn, att_mv, TT, a_mv)
            for s in range(16):
                ffn_piece(1, s, x3, x1[1])
                what = FIRST.get(s)
                if what == "LNT":
                    att_rest(0)
                elif what == "Q":
                    qk_rest(0, 0)
                elif what == "K":
                    qk_rest(0, 1)
            att_stats(1, 1)
            att_mean_var_wait(1)
            mean_var(att_bn, att_mv, TT, a_mv)
            dve.wait_ge(s_x0, 16 * 2)
            ffn_stats(x0)
            ffn_mean_var_wait(2)
            ffn_mean_var(2)

            def steps(it):
                t, par = it.t, it.par
                for s in range(UNITS):
                    norm_prep = it.prep and it.prev and s == AT_STATS_PREP + 1
                    norm_b = it.ffn_b is not None and it.prev and s == AT_STATS_B + 1
                    at_stats_a = AT_STATS_A_LAST if not it.cur else AT_STATS_A_PACED if it.pace else AT_STATS_A
                    norm_a = it.next_a is not None and s == at_stats_a + 1
                    tails = AT_STATS_TAIL if it.cur else AT_STATS_TAIL_LAST
                    norm_tail = it.prev and s - 1 in tails
                    if norm_prep:
                        att_mean_var_wait(t + 1)
                    if norm_b:
                        ffn_mean_var_wait(it.ffn_b)
                    if norm_a:
                        ffn_mean_var_wait(it.next_a)
                    if norm_tail:
                        dve.wait_ge(t_bn, 2 * (t - 1) + tails.index(s - 1) + 1)
                    for f, second, piece in ffn_rests(it, s):
                        if second:
                            ffn_piece(f, piece, x2[par], x3, stored=t - 2)
                        else:
                            ffn_piece(f, piece, x0, x1[par], based=t + 1)
                    if it.cur:
                        row_maxima(t, s)
                    if norm_prep:
                        mean_var(att_bn, att_mv, TT, a_mv)
                    if norm_b:
                        ffn_mean_var(it.ffn_b)
                    if norm_a:
                        ffn_mean_var(it.next_a)
                    if norm_tail:
                        mean_var(tail_bn, tail_mv, 2, t_mv)
                    hb = (s - HB) // HB % 4
                    split = it.prev if s == 0 else it.cur and s % HB == 0
                    split_tile = t if s else t - 1
                    if split:
                        max_hi(split_tile, hb)
                    for b in range(2):
                        if it.prev and s - 1 == at(it, f"CT{b}"):
                            context_den(t - 1, b, it.misc[f"CT{b}"])
                    if split:
                        max_lo(split_tile, hb)
                    if it.prev:
                        for b in range(2):
                            if s - 1 == at(it, f"CT{b}"):
                                context_norm(t - 1, b)
                        if s in tails:
                            tail_stats(t - 1, tails.index(s))
                    if it.prep:
                        if it.prev and s == AT_STATS_PREP:
                            att_stats(1 - par, first_ffn(t + 1))
                        if s - 1 == at(it, "LNT"):
                            att_rest(t + 1)
                        if s - 1 == at(it, "Q"):
                            qk_rest(t + 1, 0)
                        if s - 1 == at(it, "K"):
                            qk_rest(t + 1, 1)
                    if it.ffn_b is not None and it.prev and s == AT_STATS_B:
                        dve.wait_ge(s_x0, 16 * (t + 2))
                        ffn_stats(x0)
                    if it.next_a is not None and s == at_stats_a:
                        dve.wait_ge(s_x2, 2 * t)
                        ffn_stats(x2[1 - par])

            run(dve, steps)
            for s in range(16):
                ffn_piece(LAST_FFN, s, x2[(TILES - 1) % 2], x3, stored=TILES - 1)


NAMES = ["L0_attn_x", "L0_attn_Wq", "L0_attn_bq", "L0_attn_Wk", "L0_attn_bk", "L0_attn_Wv", "L0_attn_bv",
         "L0_attn_gamma", "L0_attn_beta", "L0_ffn_k0", "L0_ffn_k1", "L0_ffn_k2", "L0_ffn_s0", "L0_ffn_s1", "L0_ffn_s2"]


def kernel(**inputs):
    import concourse.bacc as bacc
    from concourse.bass_utils import run_bass_kernel_spmd

    nc = bacc.Bacc("TRN2", target_bir_lowering=False, num_devices=1)
    arrays, args = {}, []
    for name in NAMES:
        a = np.ascontiguousarray(inputs[name])
        if a.ndim == 0:
            a = a.reshape(1)
        arrays[name] = a
        args.append(nc.dram_tensor(name, a.shape, mybir.dt.from_np(a.dtype), kind="ExternalInput").ap())
    shape = inputs["L0_attn_x"].shape
    args.append(nc.dram_tensor("y", shape, F32, kind="ExternalOutput").ap())
    macaron_layer(nc, *args)
    result = run_bass_kernel_spmd(nc, [arrays], core_ids=[0])
    return result.results[0]["y"]
```
